# Optimizing a Trainium2 kernel written in Bass

```python
import numpy as np
import jax
import jax.numpy as jnp

def _softmax(x, axis=-1):
    return jax.nn.softmax(x, axis=axis)

def _gelu(x):
    return jax.nn.gelu(x, approximate=True)

def _silu(x):
    return jax.nn.silu(x)

def _sigmoid(x):
    return jax.nn.sigmoid(x)

def _layernorm(x, axis=-1, eps=1e-05):
    m = jnp.mean(x, axis=axis, keepdims=True)
    v = jnp.var(x, axis=axis, keepdims=True)
    return (x - m) / jnp.sqrt(v + eps)

def _scatter_add(tgt, idx, src, axis=0):
    return tgt.at[idx].add(src)

def _segment_sum(src, seg, n):
    return jax.ops.segment_sum(src, seg, n)
kernel_name = 'mk_xattn_seq_d1_seqx_r4_df9f0c'

def setup_inputs(seed: int=0):
    np.random.seed(seed)
    _w = jnp.asarray

    def _rec_inputs():
        import jax
        import jax.numpy as jnp
        _rk = jax.random.key(seed)
        x = -0.000296 + 1 * jax.random.normal(jax.random.fold_in(_rk, 1), (16, 256, 320), jnp.float32)
        _lenS = 256 - jax.random.randint(jax.random.fold_in(_rk, 7), (16,), 0, max(1, 256 // 4) + 1, jnp.int32)
        _lenS2 = 120 - jax.random.randint(jax.random.fold_in(_rk, 8), (16,), 0, max(1, 120 // 4) + 1, jnp.int32)
        _ctx_2048P = jax.random.normal(jax.random.fold_in(_rk, 11), (16, 16, 512), jnp.float32)
        _ctx_2048c = jax.random.dirichlet(jax.random.fold_in(_rk, 511), 0.3 * jnp.ones((16,), jnp.float32), (16, 120))
        _ctx_2048t = jnp.einsum('bsk,bkd->bsd', _ctx_2048c, _ctx_2048P)
        _ctx_2048t = _ctx_2048t * jax.lax.rsqrt(jnp.mean(jnp.square(_ctx_2048t)) + 1e-12) * 0.953939
        ctx_2048 = 0.00100794 + 0.99956 * (_ctx_2048t + 0.3 * jax.random.normal(jax.random.fold_in(_rk, 611), (16, 120, 512), jnp.float32))
        fside_S_0 = jax.random.uniform(jax.random.fold_in(_rk, 12), (256,), jnp.float32, 0.0, 0.999707)
        return (x, ctx_2048, fside_S_0)
    x, ctx_2048, fside_S_0 = _rec_inputs()

    def _L0_xattn_setup():
        import jax, jax.numpy as jnp
        import numpy as np
        import math
        HEADS = 20
        NUM_TOKENS = 4
        SEM_SCALE = 0.5
        IP_SCALE = 1.0
        TEXT_LEN = 77

        def _split_heads(x, B, H, D):
            return x.reshape(B, -1, H, D).transpose(0, 2, 1, 3)
        key = jax.random.key(seed)
        ks = jax.random.split(key, 10)
        B, S, C, CD = (4, 1024, 320, 512)

        def g(k, shape, std=1.0):
            return jax.random.normal(k, shape, dtype=jnp.float32) * std
        return {'hidden_states': g(ks[0], (B, S, C)), 'encoder_hidden_states': g(ks[1], (B, TEXT_LEN + NUM_TOKENS, CD)), 'spatial_mask': jax.random.uniform(ks[2], (S,), dtype=jnp.float32), 'Wq': g(ks[3], (C, C), 1.0 / math.sqrt(C)), 'Wk': g(ks[4], (CD, C), 1.0 / math.sqrt(CD)), 'Wv': g(ks[5], (CD, C), 1.0 / math.sqrt(CD)), 'Wk_ip': g(ks[6], (CD, C), 1.0 / math.sqrt(CD)), 'Wv_ip': g(ks[7], (CD, C), 1.0 / math.sqrt(CD)), 'Wout': g(ks[8], (C, C), 1.0 / math.sqrt(C)), 'bout': jnp.zeros((C,), dtype=jnp.float32)}
    _L0_xattn_all = _L0_xattn_setup()
    _L0_xattn_in = {k: v for k, v in _L0_xattn_all.items() if k in ('Wq', 'Wk', 'Wv', 'Wk_ip', 'Wv_ip', 'Wout', 'bout')}
    del _L0_xattn_all
    return {'x': x, 'ctx_2048': ctx_2048, 'fside_S_0': fside_S_0, 'L0_xattn_Wq': _L0_xattn_in['Wq'], 'L0_xattn_Wk': _L0_xattn_in['Wk'], 'L0_xattn_Wv': _L0_xattn_in['Wv'], 'L0_xattn_Wk_ip': _L0_xattn_in['Wk_ip'], 'L0_xattn_Wv_ip': _L0_xattn_in['Wv_ip'], 'L0_xattn_Wout': _L0_xattn_in['Wout'], 'L0_xattn_bout': _L0_xattn_in['bout']}

def reference(x, ctx_2048, fside_S_0, L0_xattn_Wq, L0_xattn_Wk, L0_xattn_Wv, L0_xattn_Wk_ip, L0_xattn_Wv_ip, L0_xattn_Wout, L0_xattn_bout):
    import jax
    import jax.numpy as jnp

    def _L0_xattn_ref(hidden_states, encoder_hidden_states, spatial_mask, Wq, Wk, Wv, Wk_ip, Wv_ip, Wout, bout):
        import jax, jax.numpy as jnp
        import numpy as np
        import math
        HEADS = 20
        NUM_TOKENS = 4
        SEM_SCALE = 0.5
        IP_SCALE = 1.0
        TEXT_LEN = 77

        def _split_heads(x, B, H, D):
            return x.reshape(B, -1, H, D).transpose(0, 2, 1, 3)
        B, S, C = hidden_states.shape
        D = C // HEADS
        scale = 1.0 / math.sqrt(D)
        residual = hidden_states
        text = encoder_hidden_states[:, :TEXT_LEN]
        ip = encoder_hidden_states[:, TEXT_LEN:]
        q = hidden_states @ Wq
        k_text = text @ Wk
        v_text = text @ Wv
        q_h = _split_heads(q, B, HEADS, D)
        k_h = _split_heads(k_text, B, HEADS, D)
        v_h = _split_heads(v_text, B, HEADS, D)
        logits = jnp.einsum('bhqd,bhkd->bhqk', q_h, k_h) * scale
        probs = jax.nn.softmax(logits, axis=-1)
        text_out = jnp.einsum('bhqk,bhkd->bhqd', probs, v_h)
        text_out = text_out.transpose(0, 2, 1, 3).reshape(B, S, C)
        ip_k = ip @ Wk_ip
        ip_v = ip @ Wv_ip
        ip_k_h = _split_heads(ip_k, B, HEADS, D)
        ip_v_h = _split_heads(ip_v, B, HEADS, D)
        scores = jnp.einsum('bhqd,bhkd->bhqk', q_h, ip_k_h) * scale
        text_probs = jax.nn.softmax(jnp.einsum('bqc,bkc->bqk', q, k_text) * scale, axis=-1)
        q_sem = jnp.einsum('bqk,bkc->bqc', text_probs, text)
        sem = jnp.einsum('bqc,bnc->bqn', q_sem, ip) * scale
        sem = jax.lax.stop_gradient(sem)
        fused = scores + SEM_SCALE * sem[:, None, :, :]
        ip_probs = jax.nn.softmax(fused, axis=-1)
        ip_probs = ip_probs * spatial_mask[None, None, :, None]
        ip_out = jnp.einsum('bhqk,bhkd->bhqd', ip_probs, ip_v_h)
        ip_out = ip_out.transpose(0, 2, 1, 3).reshape(B, S, C)
        hs = text_out + IP_SCALE * ip_out
        out = hs @ Wout + bout
        out = out + residual
        return out
    x = _L0_xattn_ref(x, ctx_2048, fside_S_0, L0_xattn_Wq, L0_xattn_Wk, L0_xattn_Wv, L0_xattn_Wk_ip, L0_xattn_Wv_ip, L0_xattn_Wout, L0_xattn_bout)
    return x

_drawn_inputs = setup_inputs


def setup_inputs(seed=0):
    import zlib

    import numpy as np

    out = dict(_drawn_inputs(seed))
    spreads = {'L0_xattn_bout': (0.0, 0.1)}
    factors = {}
    for name, (base, spread) in spreads.items():
        noise = np.random.default_rng([zlib.crc32(name.encode()), seed]).standard_normal(out[name].shape)
        drawn = base * np.exp(spread * noise) if base else spread * noise
        out[name] = jnp.asarray(drawn.astype(out[name].dtype))
    for name, factor in factors.items():
        out[name] = (out[name] * factor).astype(out[name].dtype)
    return out
```

```python
from contextlib import ExitStack

import concourse.bass as bass
from concourse import mybir

F32 = mybir.dt.float32
BF16 = mybir.dt.bfloat16
U16 = mybir.dt.uint16
ALU = mybir.AluOpType
ACT = mybir.ActivationFunctionType
AX_X = mybir.AxisListType.X

B, S, C, CD = 16, 256, 320, 512
H = 20
D = C // H
T, N = 77, 43
TOK = T + N
P = 128
PAIRS = B // 2
Q2 = 2 * S
TOK2 = 2 * TOK
KC = CD // P
CH = [(0, 8), (1, 8), (2, 4)]
ROWS = [D * nh for _, nh in CH]
TILES = Q2 // P
HG = 4
G = H // HG
GB = 4
GROUPS = B // GB
SCALE = 1.0 / D ** 0.5
SEM_SCALE = 0.5
Q_PART = [0, 0, 0, 1, 1, 2]
K_PART = [0, 1, 2, 0, 1, 0]
SLOTS = len(Q_PART)
R_QK = SLOTS * D
R_SEM = R_QK
R_MAX = R_QK + 1
R_ALL = R_MAX + 6
SEG = 2 * D
VW = H * SEG
VH = VW // 2

C_ID = 0
C_VMASK = C_ID + P
C_DEN = C_VMASK + VH
C_RIND = C_DEN + G * 32
C_COEF = C_RIND + G * P
C_END = C_COEF + 4
B_ID = 0
B_SELT = B_ID + P
B_SELQ = B_SELT + TOK
B_END = B_SELQ + HG * N


def xattn_kernel(nc, xT, xr, ctxT, fside, wq, wk, wkip, wv, wout, bout, cf, cb, krows, out):
    ctx = ExitStack()
    with ctx:
        def sb(name, shape, dt):
            return ctx.enter_context(nc.sbuf_tensor(name, shape, dt))

        def sem(name):
            return ctx.enter_context(nc.semaphore(name))

        cfs = sb("cfs", [P, C_END], F32)
        cbs = sb("cbs", [P, B_END], BF16)
        wq_sb = sb("wq_sb", [P, 3, C], F32)
        wv_sb = sb("wv_sb", [P, KC, VW], F32)
        wout_sb = sb("wout_sb", [P, G, C], F32)
        bias_sb = sb("bias_sb", [P, C], F32)
        mask_raw = sb("mask_raw", [P, S], F32)
        mask_sb = sb("mask_sb", [P, S], F32)
        ident = cfs[:, C_ID:C_ID + P]
        vmask = cfs[0:TOK, C_VMASK:C_VMASK + VH]
        den_w = cfs[0:TOK, C_DEN:C_RIND].rearrange("p (g m) -> p g m", g=G)
        r_ind = cfs[:, C_RIND:C_COEF].rearrange("p (g m) -> p g m", g=G)
        coef = cfs[:, C_COEF:C_END]
        ident_b = cbs[:, B_ID:B_ID + P]
        sel_t = cbs[:, B_SELT:B_SELT + TOK]
        sel_q = cbs[:, B_SELQ:B_END]
        weights_nums = sb("weights_nums", [P, G * Q2], F32)
        wk_sb = weights_nums[:, 0:KC * C].rearrange("p (k n) -> p k n", k=KC)
        wkip_sb = weights_nums[:, KC * C:2 * KC * C].rearrange("p (k n) -> p k n", k=KC)
        nums = weights_nums[:, :].rearrange("p (g q) -> p g q", g=G)
        ctx_hs_ob = sb("ctx_hs_ob", [P, 4 * KC * TOK2], F32)
        ctx_g = [ctx_hs_ob[:, 2 * KC * TOK2 * i:2 * KC * TOK2 * (i + 1)].rearrange("p (g k t) -> p g k t", g=2, k=KC)
                 for i in range(2)]
        hs = ctx_hs_ob[:, 0:G * Q2].rearrange("p (g q) -> p g q", g=G)
        ob = ctx_hs_ob[:, G * Q2:G * Q2 + TILES * C].rearrange("p (t n) -> p t n", t=TILES)
        rest = [sb(f"rest{i}", [P, Q2], F32) for i in range(2)]
        k_parts = sb("k_parts", [P, 3, 3, B * TOK], BF16)
        xT_sb = sb("xT_sb", [P, 3, Q2], F32)
        ctx_sb = sb("ctx_sb", [P, KC, TOK2], F32)
        xr_sb = sb("xr_sb", [P, TILES, C], F32)
        q_parts = sb("q_parts", [P, 3, 3, Q2], BF16)
        qpack = [sb(f"qpack{i}", [R_ALL, H, Q2], BF16) for i in range(2)]
        kpack = [sb(f"kpack{i}", [R_ALL, H, TOK2], BF16) for i in range(2)]
        v_sb = [[sb(f"v_sb{i}{u}", [TOK, VW], F32) for u in range(2)] for i in range(2)]
        sempack = [sb(f"sempack{i}", [P, Q2], BF16) for i in range(2)]
        g_sb = [sb(f"g_sb{u}", [T, 3, N], F32) for u in range(2)]
        sem_low = sb("sem_low", [P, Q2], BF16)
        sem_hi = sb("sem_hi", [P, Q2], BF16)
        sem_mid = sem_hi
        sem_rest = sb("sem_rest", [P, Q2], F32)
        l_max = sb("l_max", [P, TILES], F32)
        l_den = sb("l_den", [P, TILES], F32)
        l_rec = sb("l_rec", [P, TILES], F32)
        l_exp = sb("l_exp", [P, TILES, T], F32)
        pT_sb = sb("pT_sb", [T, Q2], F32)
        m_neg = sb("m_neg", [P, TILES, 2 * H], F32)
        m_rest = sb("m_rest", [P, TILES, 2 * H], F32)
        m_parts = sb("m_parts", [P, TILES, 3, 2 * H], BF16)
        mT_sb = sb("mT_sb", [6 * H, Q2], BF16)
        pt = [sb(f"pt{i}", [TOK, HG, S], F32) for i in range(2)]
        rec = sb("rec", [P, Q2], F32)

        bank = [ctx.enter_context(nc.psum_tensor(f"bank{i}", [P, 512], F32)) for i in range(8)]
        PJ = bank[0:2]
        SQ = bank[2:4]
        ST = bank[4:6]
        NU = bank[6]
        DE = bank[7]

        d_const, d_wk, d_w, d_ctx_g = sem("d_const"), sem("d_wk"), sem("d_w"), [sem("d_ctx_g0"), sem("d_ctx_g1")]
        d_xT, d_ctx, d_xr = sem("d_xT"), sem("d_ctx"), sem("d_xr")
        d_pack, d_mrow, d_semrow, d_out = sem("d_pack"), sem("d_mrow"), sem("d_semrow"), sem("d_out")
        k_mm, k_hi, k_rs, k_mid, k_low = (sem(n) for n in ("k_mm", "k_hi", "k_rs", "k_mid", "k_low"))
        q_mm, q_hi, q_rs, q_mid, q_low = (sem(n) for n in ("q_mm", "q_hi", "q_rs", "q_mid", "q_low"))
        v_mm, v_done, g_done = sem("v_mm"), sem("v_done"), sem("g_done")
        l_mm, l_maxed, l_exped, l_normed = sem("l_mm"), sem("l_maxed"), sem("l_exped"), sem("l_normed")
        l_recip = sem("l_recip")
        pT_mm, pT_done, sem_mm = sem("pT_mm"), sem("pT_done"), sem("sem_mm")
        s_hi, s_rest, s_mid, s_pack, s_low = (sem(n) for n in ("s_hi", "s_rest", "s_mid", "s_pack", "s_low"))
        sq_mm, sq_max = sem("sq_mm"), sem("sq_max")
        m_step, m_split, mT_mm, mT_done = sem("m_step"), sem("m_split"), sem("mT_mm"), sem("mT_done")
        st_mm, exped, pv_mm, nu_done = sem("st_mm"), sem("exped"), sem("pv_mm"), sem("nu_done")
        de_read, rec_done, r_mm, hs_done = sem("de_read"), sem("rec_done"), sem("r_mm"), sem("hs_done")
        o_mm, o_done, xb_done = sem("o_mm"), sem("o_done"), sem("xb_done")
        mask_set = sem("mask_set")

        N_SQ = TILES * G
        N_PV = 2 * G
        N_ST = 2 * N_PV
        D_PACK = 16 * 2 * 3 * SLOTS

        block = ctx.enter_context(nc.Block())

        def need(eng, s, value):
            if isinstance(value, int) and value <= 0:
                return
            eng.wait_ge(s, value)

        def run(eng, iteration):
            iteration(-1, 1, False, False, True)
            iteration(0, 0, False, True, True)
            iteration(1, 1, True, True, True)
            with eng.Fori(0, PAIRS // 2 - 2) as i:
                iteration(2 * i + 2, 0, True, True, True)
                iteration(2 * i + 3, 1, True, True, True)
            iteration(PAIRS - 2, 0, True, True, True)
            iteration(PAIRS - 1, 1, True, True, False)
            iteration(PAIRS, 0, True, False, False)

        @block.sync
        def _(sp):
            for k in range(KC):
                sp.dma_start(wk_sb[:, k, :], wk[k]).then_inc(d_wk, 16)
            sp.dma_start(ctx_g[0], ctxT[0:2].rearrange("g p k t -> p g k t")).then_inc(d_ctx_g[0], 16)
            for k in range(KC):
                sp.dma_start(wkip_sb[:, k, :], wkip[k]).then_inc(d_wk, 16)
            sp.dma_start(ctx_g[1], ctxT[2:4].rearrange("g p k t -> p g k t")).then_inc(d_ctx_g[1], 16)
            sp.dma_start(cfs[:], cf).then_inc(d_const, 16)
            sp.dma_start(cbs[:].bitcast(U16), cb).then_inc(d_const, 16)
            for i in range(2):
                sp.dma_start(kpack[i][R_SEM:R_ALL, :, :].bitcast(U16), krows).then_inc(d_const, 16)
            sp.dma_start(mask_raw[:], fside.rearrange("(a s) -> a s", a=1).broadcast_to((P, S))).then_inc(d_const, 16)
            sp.dma_start(bias_sb[:], bout.rearrange("(a s) -> a s", a=1).broadcast_to((P, C))).then_inc(d_const, 16)
            sp.dma_start(wq_sb[:], wq.rearrange("(c p) n -> p c n", p=P)).then_inc(d_w, 16)
            for k in range(KC):
                sp.dma_start(wv_sb[:, k, :], wv[k]).then_inc(d_w, 16)
            sp.dma_start(wout_sb[:], wout.rearrange("g p n -> p g n")).then_inc(d_w, 16)
            for g in range(2, GROUPS):
                sp.wait_ge(k_mm, 3 * (g - 1))
                sp.dma_start(ctx_g[g % 2], ctxT[2 * g:2 * g + 2].rearrange("g p k t -> p g k t")).then_inc(
                    d_ctx_g[g % 2], 16)

            def iteration(j, q, old, cur, nxt):
                more = not isinstance(j, int) or j + 2 < PAIRS
                if not old and not cur:
                    sp.dma_start(xT_sb[:], xT[0].rearrange("c p q -> p c q")).then_inc(d_xT, 16)
                    sp.dma_start(ctx_sb[:], ctxT[0]).then_inc(d_ctx, 16)
                if nxt:
                    if not old and not cur:
                        sp.wait_ge(k_low, 3 * GROUPS)
                    for c, nh in CH:
                        if old:
                            sp.wait_ge(st_mm, N_ST * (j - 1) + min(8 * (c + 1), N_ST))
                        for s in range(SLOTS):
                            sp.dma_start(kpack[q ^ 1][D * s:D * (s + 1), 8 * c:8 * c + nh, :],
                                         k_parts[0:D * nh, c, K_PART[s], bass.ds(TOK2 * (j + 1), TOK2)]).then_inc(
                                             d_pack, 16)
                        need(sp, q_low, 3 * (j + 1) + c + 1)
                        for s in range(SLOTS):
                            sp.dma_start(qpack[q ^ 1][D * s:D * (s + 1), 8 * c:8 * c + nh, :],
                                         q_parts[0:D * nh, c, Q_PART[s], :]).then_inc(d_pack, 16)
                if nxt and more:
                    need(sp, q_mm, 3 * (j + 2))
                    sp.dma_start(xT_sb[:], xT[j + 2].rearrange("c p q -> p c q")).then_inc(d_xT, 16)
                if cur:
                    need(sp, mT_done, j + 1)
                    sp.dma_start(qpack[q][R_MAX:R_ALL, :, :], mT_sb[:, :]).then_inc(d_mrow, 16)
                if nxt and more:
                    need(sp, v_mm, 4 * (j + 2))
                    sp.dma_start(ctx_sb[:], ctxT[j + 2]).then_inc(d_ctx, 16)
                if nxt:
                    need(sp, s_low, j + 2)
                    sp.dma_start(qpack[q ^ 1][R_SEM:R_SEM + 1, :, :],
                                 sem_low[2 * N - 1:2 * N, :].unsqueeze(1).broadcast_to((1, H, Q2))).then_inc(
                                     d_semrow, 16)
                if old:
                    need(sp, o_done, TILES * j)
                    sp.dma_start(out[j - 1], ob).then_inc(d_out, 16)
                if cur:
                    need(sp, o_done, TILES * j)
                    sp.dma_start(xr_sb[:], xr[j]).then_inc(d_xr, 16)

            run(sp, iteration)
            sp.wait_ge(d_out, 16 * PAIRS)

        @block.tensor
        def _(pe):
            def key_group(g, i):
                pe.wait_ge(d_ctx_g[i], 16 * (g // 2 + 1) if isinstance(g, int) else 8 * (g - i) + 16)
                for c, nh in CH:
                    nr = D * nh
                    b = PJ[(3 * i + c) % 2]
                    if not (isinstance(g, int) and 3 * g + c - 1 <= 0):
                        pe.wait_ge(k_rs, 3 * g + c - 1)
                    ps = b[0:nr, 0:GB * TOK].rearrange("p (g b t) -> p g b t", g=2, b=2)
                    cg = ctx_g[i].rearrange("p g k (b t) -> p g k b t", b=2)
                    for w, t0, t1 in ((wk_sb, 0, T), (wkip_sb, T, TOK)):
                        for k in range(KC):
                            mm = pe.matmul(ps[:, :, :, t0:t1], w[:, k, P * c:P * c + nr], cg[:, :, k, :, t0:t1],
                                           start=(k == 0), stop=(k == KC - 1), skip_group_check=True)
                    mm.then_inc(k_mm, 1)

            pe.wait_ge(d_wk, 16 * 2 * KC)
            for g in range(GROUPS):
                key_group(g, g % 2)

            def queries(j, c):
                nr = ROWS[c]
                if c == 0:
                    pe.wait_ge(d_xT, 16 * (j + 2))
                    if not isinstance(j, int) or j >= 0:
                        pe.wait_ge(s_rest, j + 1)
                if c == 1 and (not isinstance(j, int) or j >= 0):
                    need(pe, pT_done, j + 1)
                    need(pe, mT_done, j)
                if c == 2:
                    need(pe, q_rs, 3 * (j + 1) + 1)
                for k in range(3):
                    mm = pe.matmul(PJ[c % 2][0:nr, :], wq_sb[:, k, P * c:P * c + nr], xT_sb[:, k, :],
                                   start=(k == 0), stop=(k == 2))
                mm.then_inc(q_mm, 1)

            def values(j, u):
                if u == 0:
                    pe.wait_ge(d_ctx, 16 * (j + 2))
                    need(pe, q_rs, 3 * (j + 2))
                else:
                    need(pe, v_done, 4 * (j + 1) + 2)
                    need(pe, g_done, 2 * (j + 1) + 1)
                for half in range(2):
                    for k in range(KC):
                        lhs = ctx_sb[:, k, TOK * u:TOK * (u + 1)]
                        mm = pe.matmul(PJ[half][0:TOK, 0:VH], lhs, wv_sb[:, k, VH * half:VH * (half + 1)],
                                       start=(k == 0), stop=(k == KC - 1), skip_group_check=True)
                        if half == 1:
                            mm = pe.matmul(PJ[1][0:TOK, VH:VH + N], lhs, ctx_sb[:, k, TOK * u + T:TOK * (u + 1)],
                                           start=False, stop=(k == KC - 1), skip_group_check=True)
                    mm.then_inc(v_mm, 1)

            def text_logits(j, q):
                pe.wait_ge(d_pack, D_PACK * (j + 2))
                need(pe, v_done, 4 * (j + 2) - 1)
                for t in range(TILES):
                    for h in range(H):
                        mm = pe.matmul(PJ[0][:, T * t:T * (t + 1)], qpack[q ^ 1][0:R_QK, h, P * t:P * (t + 1)],
                                       kpack[q ^ 1][0:R_QK, h, TOK * (t // 2):TOK * (t // 2) + T],
                                       start=(h == 0), stop=(h == H - 1), skip_group_check=True)
                mm.then_inc(l_mm, 1)

            def text_probs_T(j):
                need(pe, l_normed, j + 2)
                need(pe, g_done, 2 * (j + 2))
                need(pe, v_done, 4 * (j + 2))
                if not isinstance(j, int) or j >= 0:
                    need(pe, mT_done, j + 1)
                for t in range(TILES):
                    mm = pe.transpose(PJ[1][0:T, P * t:P * (t + 1)], l_exp[:, t, :], ident)
                mm.then_inc(pT_mm, 1)

            def semantic(j):
                need(pe, pT_done, j + 2)
                for u in range(2):
                    mm = pe.matmul(PJ[0][:, S * u:S * (u + 1)], g_sb[u][:].rearrange("p r n -> p (r n)")[:, 0:P],
                                   pT_sb[:, S * u:S * (u + 1)], start=True, stop=True, skip_group_check=True)
                mm.then_inc(sem_mm, 1)

            def rows(j, q, n):
                t, g = divmod(n, G)
                b = SQ[n % 2]
                if n == 0:
                    need(pe, s_pack, j + 1)
                if n < 2:
                    need(pe, o_done, TILES * (j - 1))
                need(pe, sq_max, N_SQ * j + n - 1)
                for i in range(HG):
                    pe.matmul(b[:, TOK * i:TOK * (i + 1)], qpack[q][0:R_QK, HG * g + i, P * t:P * (t + 1)],
                              kpack[q][0:R_QK, HG * g + i, TOK * (t // 2):TOK * (t // 2 + 1)],
                              start=(i == 0), stop=False, skip_group_check=True)
                ip = b[:, 0:HG * TOK].rearrange("p (h t) -> p h t", h=HG)[:, :, T:TOK]
                pe.matmul(ip, sempack[q][:, P * t:P * (t + 1)], sel_q.rearrange("p (h n) -> p h n", h=HG),
                          start=False, stop=True, skip_group_check=True).then_inc(sq_mm, 1)

            def maxima_T(j):
                need(pe, m_split, j + 1)
                for t in range(TILES):
                    mm = pe.transpose(PJ[1].bitcast(BF16)[0:6 * H, P * t:P * (t + 1)],
                                      m_parts[:, t, :, :].rearrange("p a b -> p (a b)"), ident_b)
                mm.then_inc(mT_mm, 1)

            def columns(j, q, n):
                g, u = divmod(n, 2)
                if n == 0:
                    need(pe, d_mrow, 16 * j)
                    need(pe, d_semrow, 16 * j)
                for i in range(2):
                    if n == 0:
                        need(pe, hs_done, G * (j - 1))
                    else:
                        need(pe, exped, N_ST * (j - 1) + 2 * n + i - 1)
                    pe.matmul(ST[i][0:TOK, :].rearrange("p (h q) -> p h q", h=2), sel_t,
                              sempack[q ^ 1][:, S * u:S * (u + 1)].unsqueeze(1).broadcast_to((P, 2, S)),
                              start=True, stop=False, skip_group_check=True)
                    for k in range(2):
                        h = HG * g + 2 * i + k
                        mm = pe.matmul(ST[i][0:TOK, S * k:S * (k + 1)], kpack[q ^ 1][:, h, TOK * u:TOK * (u + 1)],
                                       qpack[q ^ 1][:, h, S * u:S * (u + 1)],
                                       start=False, stop=(k == 1), skip_group_check=True)
                    mm.then_inc(st_mm, 1)

            def value_products(j, q, n):
                g, u = divmod(n, 2)
                need(pe, exped, N_ST * (j - 1) + 2 * n + 2)
                if n == 0:
                    need(pe, de_read, j - 1)
                for i in range(HG):
                    pe.matmul(DE[32 * i:32 * (i + 1), S * u:S * (u + 1)], den_w[:, g, :], pt[n % 2][:, i, :],
                              start=(n == 0), stop=(g == G - 1), skip_group_check=True)
                need(pe, nu_done, N_PV * (j - 1) + n)
                for i in range(HG):
                    h = HG * g + i
                    mm = pe.matmul(NU[32 * i:32 * (i + 1), 0:S], v_sb[q ^ 1][u][:, SEG * h:SEG * (h + 1)],
                                   pt[n % 2][:, i, :], start=True, stop=True)
                mm.then_inc(pv_mm, 1)

            def scales(j, g):
                if g == 0:
                    need(pe, rec_done, j)
                if g >= 2:
                    need(pe, hs_done, G * (j - 1) + g - 1)
                pe.matmul(ST[g % 2][:, :], r_ind[:, g, :], rec[:, :], start=True, stop=True).then_inc(r_mm, 1)

            def project(j, t):
                if t == 0:
                    need(pe, hs_done, G * j)
                    if not isinstance(j, int) or j < PAIRS:
                        need(pe, sq_max, N_SQ * (j + 1))
                    need(pe, o_done, TILES * (j - 1))
                if t >= 2:
                    need(pe, o_done, TILES * (j - 1) + t - 1)
                for g in range(G):
                    mm = pe.matmul(SQ[t % 2][:, 0:C], hs[:, g, P * t:P * (t + 1)], wout_sb[:, g, :],
                                   start=(g == 0), stop=(g == G - 1))
                mm.then_inc(o_mm, 1)

            pe.wait_ge(d_const, 16 * 6)
            pe.wait_ge(d_w, 16 * (2 + KC))
            pe.wait_ge(k_rs, 3 * GROUPS)

            def iteration(j, q, old, cur, nxt):
                for n in range(N_PV):
                    if old:
                        columns(j, q, n)
                    if cur:
                        rows(j, q, 2 * n)
                        rows(j, q, 2 * n + 1)
                    if old and n:
                        value_products(j, q, n - 1)
                    if nxt and n in (1, 4, 7):
                        queries(j, n // 3)
                if old:
                    value_products(j, q, N_PV - 1)
                if nxt:
                    values(j, 0)
                if old:
                    for g in range(G):
                        scales(j, g)
                if cur:
                    if nxt:
                        need(pe, g_done, 2 * (j + 1) + 1)
                    maxima_T(j)
                if nxt:
                    if cur:
                        need(pe, mT_done, j + 1)
                    values(j, 1)
                    text_logits(j, q)
                if old:
                    project(j, 0)
                    project(j, 1)
                if nxt:
                    text_probs_T(j)
                if old:
                    project(j, 2)
                if nxt:
                    semantic(j)
                if old:
                    project(j, 3)

            run(pe, iteration)

        @block.scalar
        def _(act):
            for g in range(GROUPS):
                for c, nh in CH:
                    nr, n = D * nh, 3 * g + c
                    act.wait_ge(k_mm, n + 1)
                    act.activation(k_parts[0:nr, c, 0, GB * TOK * g:GB * TOK * (g + 1)], PJ[n % 2][0:nr, 0:GB * TOK],
                                   ACT.Copy).then_inc(k_hi, 1)
                    act.wait_ge(k_rs, n + 1)
                    act.activation(k_parts[0:nr, c, 1, GB * TOK * g:GB * TOK * (g + 1)], rest[n % 2][0:nr, 0:GB * TOK],
                                   ACT.Copy).then_inc(k_mid, 1)

            def q_high(j, c):
                nr = ROWS[c]
                if c == 0:
                    need(act, d_pack, D_PACK * (j + 1))
                need(act, q_mm, 3 * (j + 1) + c + 1)
                act.activation(q_parts[0:nr, c, 0, :], PJ[c % 2][0:nr, :], ACT.Copy, scale=SCALE).then_inc(q_hi, 1)

            def q_middle(j, c):
                nr = ROWS[c]
                need(act, q_rs, 3 * (j + 1) + c + 1)
                act.activation(q_parts[0:nr, c, 1, :], rest[c % 2][0:nr, :], ACT.Copy).then_inc(q_mid, 1)

            def softmax_exp(j, n):
                if n >= 2:
                    need(act, pv_mm, N_PV * (j - 1) + n - 1)
                for i in range(2):
                    need(act, st_mm, N_ST * (j - 1) + 2 * n + i + 1)
                    act.activation(pt[n % 2][:, 2 * i:2 * i + 2, :].rearrange("p h q -> p (h q)"), ST[i][0:TOK, :],
                                   ACT.Exp).then_inc(exped, 1)

            def nums_out(j, n):
                g, u = divmod(n, 2)
                need(act, pv_mm, N_PV * (j - 1) + n + 1)
                if n == 0:
                    need(act, hs_done, G * (j - 1))
                act.activation(nums[:, g, S * u:S * (u + 1)], NU[:, 0:S], ACT.Copy).then_inc(nu_done, 1)

            def g_out(j, u):
                if u == 0:
                    need(act, sem_mm, j + 1)
                need(act, v_done, 4 * (j + 1) + 2 * u + 2)
                act.activation(g_sb[u][:], PJ[1][0:T, VH:VH + N].unsqueeze(1).broadcast_to((T, 3, N)), ACT.Copy,
                               scale=SCALE * SEM_SCALE).then_inc(g_done, 1)

            def iteration(j, q, old, cur, nxt):
                for n in range(N_PV):
                    if old:
                        softmax_exp(j, n)
                        if n:
                            nums_out(j, n - 1)
                    if nxt and n in (1, 4, 7):
                        q_high(j, n // 3)
                    if nxt and n in (2, 5, 8):
                        q_middle(j, n // 3)
                if old:
                    nums_out(j, N_PV - 1)
                if nxt:
                    g_out(j, 0)
                if cur:
                    need(act, mT_mm, j + 1)
                    need(act, d_mrow, 16 * j)
                    act.activation(mT_sb[:, :], PJ[1].bitcast(BF16)[0:6 * H, 0:Q2], ACT.Copy).then_inc(mT_done, 1)
                if nxt:
                    g_out(j, 1)
                    need(act, l_maxed, j + 2)
                    need(act, l_normed, j + 1)
                    for t in range(TILES):
                        act.activation(l_exp[:, t, :], PJ[0][:, T * t:T * (t + 1)], ACT.Exp, bias=l_max[:, t:t + 1],
                                       accum_out=l_den[:, t:t + 1]).then_inc(l_exped, 1)
                    need(act, pT_mm, j + 2)
                    need(act, sem_mm, j + 1)
                    act.activation(pT_sb[:, :], PJ[1][0:T, :], ACT.Copy).then_inc(pT_done, 1)
                    need(act, sem_mm, j + 2)
                    need(act, s_pack, j + 1)
                    need(act, s_low, j + 1)
                    act.activation(sem_hi[:, :], PJ[0][:, :], ACT.Copy).then_inc(s_hi, 1)
                    need(act, s_rest, j + 2)
                    act.activation(sem_mid[:, :], sem_rest[:, :], ACT.Copy).then_inc(s_mid, 1)

            run(act, iteration)

        @block.vector
        def _(dve):
            dve.wait_ge(d_const, 16 * 6)
            dve.tensor_scalar(mask_sb[:, :], mask_raw[:, :], coef[:, 2:3], coef[:, 3:4], ALU.mult,
                              ALU.add).then_inc(mask_set, 1)
            for g in range(GROUPS):
                for c, nh in CH:
                    nr, n = D * nh, 3 * g + c
                    dve.wait_ge(k_hi, n + 1)
                    need(dve, k_low, n - 1)
                    dve.tensor_tensor(rest[n % 2][0:nr, 0:GB * TOK], PJ[n % 2][0:nr, 0:GB * TOK],
                                      k_parts[0:nr, c, 0, GB * TOK * g:GB * TOK * (g + 1)],
                                      ALU.subtract).then_inc(k_rs, 1)

            def row_max(j, n):
                t, g = divmod(n, G)
                need(dve, sq_mm, N_SQ * j + n + 1)
                if n == 0:
                    need(dve, m_split, j)
                b = SQ[n % 2][:, 0:HG * TOK].rearrange("p (h t) -> p h t", h=HG)
                dve.tensor_reduce(m_neg[:, t, HG * g:HG * (g + 1)], b[:, :, 0:T], AX_X, ALU.max, negate=True)
                dve.tensor_reduce(m_neg[:, t, H + HG * g:H + HG * (g + 1)], b[:, :, T:TOK], AX_X, ALU.max,
                                  negate=True).then_inc(sq_max, 1)

            def split_maxima(j):
                need(dve, sq_max, N_SQ * (j + 1))
                need(dve, mT_mm, j)
                dve.tensor_copy(m_parts[:, :, 0, :], m_neg[:, :, :]).then_inc(m_step, 1)
                need(dve, m_step, 3 * j + 1)
                dve.tensor_tensor(m_rest[:, :, :], m_neg[:, :, :], m_parts[:, :, 0, :],
                                  ALU.subtract).then_inc(m_step, 1)
                need(dve, m_step, 3 * j + 2)
                dve.tensor_copy(m_parts[:, :, 1, :], m_rest[:, :, :]).then_inc(m_step, 1)
                need(dve, m_step, 3 * j + 3)
                dve.tensor_tensor(m_parts[:, :, 2, :], m_rest[:, :, :], m_parts[:, :, 1, :],
                                  ALU.subtract).then_inc(m_split, 1)

            def q_remainder(j, c):
                nr = ROWS[c]
                need(dve, q_hi, 3 * (j + 1) + c + 1)
                need(dve, q_low, 3 * (j + 1) + c - 1)
                dve.scalar_tensor_tensor(rest[c % 2][0:nr, :], PJ[c % 2][0:nr, :], SCALE, q_parts[0:nr, c, 0, :],
                                         ALU.mult, ALU.subtract).then_inc(q_rs, 1)

            def values_out(j, q, u):
                for half in range(2):
                    need(dve, v_mm, 4 * (j + 1) + 2 * u + half + 1)
                    dve.tensor_tensor(v_sb[q ^ 1][u][:, VH * half:VH * (half + 1)], PJ[half][0:TOK, 0:VH], vmask,
                                      ALU.mult).then_inc(v_done, 1)

            def output(j, t):
                if t == 0:
                    need(dve, d_out, 16 * (j - 1))
                    need(dve, xb_done, j)
                need(dve, o_mm, TILES * (j - 1) + t + 1)
                dve.tensor_tensor(ob[:, t, :], SQ[t % 2][:, 0:C], xr_sb[:, t, :], ALU.add).then_inc(o_done, 1)

            def iteration(j, q, old, cur, nxt):
                for n in range(N_PV):
                    if cur:
                        row_max(j, 2 * n)
                        row_max(j, 2 * n + 1)
                    if nxt and n in (1, 4, 7):
                        q_remainder(j, n // 3)
                if cur:
                    split_maxima(j)
                if old:
                    need(dve, pv_mm, N_PV * j)
                    need(dve, r_mm, G * (j - 1))
                    dve.reciprocal(rec[:, :], DE[:, :]).then_inc(de_read, 1)
                    need(dve, de_read, j)
                    if isinstance(j, int) and j == 1 or not isinstance(j, int):
                        dve.wait_ge(mask_set, 1)
                    r2 = rec[:, :].rearrange("p (u q) -> p u q", u=2)
                    dve.tensor_tensor(r2, r2, mask_sb[:, :].unsqueeze(1).broadcast_to((P, 2, S)),
                                      ALU.mult).then_inc(rec_done, 1)
                if nxt:
                    values_out(j, q, 0)
                if old:
                    need(dve, nu_done, N_PV * j)
                    need(dve, o_mm, TILES * (j - 1))
                    for g in range(G):
                        need(dve, r_mm, G * (j - 1) + g + 1)
                        dve.tensor_tensor(hs[:, g, :], ST[g % 2][:, :], nums[:, g, :], ALU.mult).then_inc(hs_done, 1)
                if nxt:
                    values_out(j, q, 1)
                    need(dve, l_mm, j + 2)
                    dve.tensor_reduce(l_max[:, :], PJ[0][:, 0:TILES * T].rearrange("p (t k) -> p t k", t=TILES), AX_X,
                                      ALU.max, negate=True).then_inc(l_maxed, 1)
                if nxt:
                    need(dve, l_exped, TILES * (j + 2))
                    dve.reciprocal(l_rec[:, :], l_den[:, :]).then_inc(l_recip, 1)
                    need(dve, l_recip, j + 2)
                    need(dve, pT_mm, j + 1)
                    dve.tensor_tensor(l_exp[:, :, :], l_exp[:, :, :],
                                      l_rec[:, :].unsqueeze(2).broadcast_to((P, TILES, T)), ALU.mult).then_inc(l_normed, 1)
                if old:
                    output(j, 0)
                    output(j, 1)
                    output(j, 2)
                if nxt:
                    need(dve, s_hi, j + 2)
                    need(dve, s_pack, j + 1)
                    need(dve, s_low, j + 1)
                    dve.scalar_tensor_tensor(sem_rest[:, :], sem_hi[:, :], coef[:, 0:1], PJ[0][:, :], ALU.mult,
                                             ALU.add).then_inc(s_rest, 1)
                if nxt:
                    need(dve, s_mid, j + 2)
                    need(dve, s_rest, j + 2)
                    dve.scalar_tensor_tensor(sempack[q ^ 1][:, :], sem_mid[:, :], coef[:, 1:2], sem_rest[:, :],
                                             ALU.mult, ALU.add).then_inc(s_pack, 1)
                if old:
                    output(j, 3)

            dve.wait_ge(k_low, 3 * GROUPS)
            run(dve, iteration)

        @block.gpsimd
        def _(pool):
            for g in range(GROUPS):
                for c, nh in CH:
                    nr, n = D * nh, 3 * g + c
                    pool.wait_ge(k_mid, n + 1)
                    pool.tensor_tensor(k_parts[0:nr, c, 2, GB * TOK * g:GB * TOK * (g + 1)], rest[n % 2][0:nr, 0:GB * TOK],
                                       k_parts[0:nr, c, 1, GB * TOK * g:GB * TOK * (g + 1)],
                                       ALU.subtract).then_inc(k_low, 1)
            pool.wait_ge(d_const, 16 * 6)

            def iteration(j, q, old, cur, nxt):
                if nxt:
                    for c in range(3):
                        nr = ROWS[c]
                        need(pool, q_mid, 3 * (j + 1) + c + 1)
                        pool.tensor_tensor(q_parts[0:nr, c, 2, :], rest[c % 2][0:nr, :], q_parts[0:nr, c, 1, :],
                                           ALU.subtract).then_inc(q_low, 1)
                if nxt:
                    need(pool, s_mid, j + 2)
                    need(pool, d_semrow, 16 * (j + 1))
                    pool.tensor_tensor(sem_low[:, :], sem_rest[:, :], sem_mid[:, :], ALU.subtract).then_inc(s_low, 1)
                if cur:
                    need(pool, d_xr, 16 * (j + 1))
                    pool.tensor_tensor(xr_sb[:, :, :], xr_sb[:, :, :],
                                       bias_sb[:, :].unsqueeze(1).broadcast_to((P, TILES, C)),
                                       ALU.add).then_inc(xb_done, 1)

            run(pool, iteration)


def constants():
    import numpy as np

    f = np.zeros((P, C_END), np.float32)
    f[:, C_ID:C_ID + P] = np.eye(P)
    vm = f[:, C_VMASK:C_VMASK + VH].reshape(P, H // 2, 2, D)
    vm[0:T, :, 0, :] = 1.0
    vm[T:TOK, :, 1, :] = 1.0
    dw = f[:, C_DEN:C_RIND].reshape(P, G, 32)
    for g in range(G):
        dw[0:T, g, 2 * g] = 1.0
        dw[T:TOK, g, 2 * g + 1] = 1.0
    dw[0:TOK, 0, 2 * G:] = 1.0
    ri = f[:, C_RIND:C_COEF].reshape(P, G, P)
    for i in range(HG):
        for g in range(G):
            for e in range(2):
                ri[32 * i + 2 * g + e, g, 32 * i + D * e:32 * i + D * (e + 1)] = 1.0
    f[N:, C_COEF] = -1.0
    f[2 * N:, C_COEF + 1] = -1.0
    row = np.arange(P) % 32
    is_ip = (row < 2 * G) & (row % 2 == 1)
    f[:, C_COEF + 2] = is_ip
    f[:, C_COEF + 3] = ~is_ip

    b = np.zeros((P, B_END), np.float32)
    b[:, B_ID:B_ID + P] = np.eye(P)
    for r in range(P):
        b[r, B_SELT + T + r % N] = 1.0
        for i in range(HG):
            b[r, B_SELQ + N * i + r % N] = 1.0
    k = np.zeros((R_ALL - R_SEM, H, 2, TOK), np.float32)
    k[0, :, :, TOK - 1] = 1.0
    for part in range(3):
        k[1 + 2 * part, :, :, 0:T] = 1.0
        k[2 + 2 * part, :, :, T:TOK] = 1.0
    return f, (b.view(np.uint32) >> 16).astype(np.uint16), (
        k.reshape(-1, H, TOK2).view(np.uint32) >> 16).astype(np.uint16)


def kernel(**inputs):
    import numpy as np
    import concourse.bacc as bacc
    from concourse.bass_utils import run_bass_kernel_spmd

    a = {k: np.asarray(v) for k, v in inputs.items()}

    def by_chunk(w):
        return np.concatenate([w[:, P * c:P * c + D * nh].reshape(-1, nh, D).transpose(0, 2, 1).reshape(-1, D * nh)
                               for c, nh in CH], 1)

    x = a["x"]
    xT = x.reshape(PAIRS, Q2, C).transpose(0, 2, 1)
    xT = np.pad(xT, ((0, 0), (0, 3 * P - C), (0, 0))).reshape(PAIRS, 3, P, Q2)
    xr = x.reshape(PAIRS, TILES, P, C).transpose(0, 2, 1, 3)
    ctxT = a["ctx_2048"].reshape(PAIRS, TOK2, KC, P).transpose(0, 3, 2, 1)
    wv = np.stack([a["L0_xattn_Wv"].reshape(CD, H, D), a["L0_xattn_Wv_ip"].reshape(CD, H, D)], 2)
    wo = a["L0_xattn_Wout"].reshape(G, HG, 1, D, C)
    wo = np.concatenate([wo, wo], 2).reshape(G, P, C)
    f, b, k = constants()
    arrays = {
        "xT": xT, "xr": xr, "ctxT": ctxT, "fside": a["fside_S_0"],
        "wq": np.pad(by_chunk(a["L0_xattn_Wq"]), ((0, 3 * P - C), (0, 0))),
        "wk": by_chunk(a["L0_xattn_Wk"]).reshape(KC, P, C),
        "wkip": by_chunk(a["L0_xattn_Wk_ip"]).reshape(KC, P, C),
        "wv": wv.reshape(KC, P, VW), "wout": wo, "bout": a["L0_xattn_bout"],
        "cf": f, "cb": b, "krows": k,
    }
    arrays = {n: np.ascontiguousarray(v) for n, v in arrays.items()}
    nc = bacc.Bacc("TRN2", target_bir_lowering=False, num_devices=1)
    args = [nc.dram_tensor(n, v.shape, mybir.dt.from_np(v.dtype), kind="ExternalInput").ap()
            for n, v in arrays.items()]
    out = nc.dram_tensor("out", (PAIRS, P, TILES, C), F32, kind="ExternalOutput").ap()
    xattn_kernel(nc, *args, out)
    r = run_bass_kernel_spmd(nc, [arrays], core_ids=[0])
    return r.results[0]["out"].transpose(0, 2, 1, 3).reshape(B, S, C)
```

```python
from contextlib import ExitStack

import concourse.bass as bass
from concourse import mybir

F32 = mybir.dt.float32
BF16 = mybir.dt.bfloat16
U16 = mybir.dt.uint16
ALU = mybir.AluOpType
ACT = mybir.ActivationFunctionType
AX_X = mybir.AxisListType.X

B, S, C, CD = 16, 256, 320, 512
H = 20
D = C // H
T, N = 77, 43
TOK = T + N
P = 128
PAIRS = B // 2
Q2 = 2 * S
TOK2 = 2 * TOK
KC = CD // P
CH = [(0, 8), (1, 8), (2, 4)]
ROWS = [D * nh for _, nh in CH]
TILES = Q2 // P
HG = 4
G = H // HG
GB = 4
GROUPS = B // GB
SCALE = 1.0 / D ** 0.5
SEM_SCALE = 0.5
Q_PART = [0, 0, 0, 1, 1, 2]
K_PART = [0, 1, 2, 0, 1, 0]
SLOTS = len(Q_PART)
R_QK = SLOTS * D
R_SEM = R_QK
R_MAX = R_QK + 1
R_ALL = R_MAX + 6
SEG = 2 * D
VW = H * SEG
VG = [(G + 1) // 2, G // 2]
VH = [HG * SEG * n for n in VG]
CHUNKS = VG[0]
STEPS = [(g, u) for c in range(CHUNKS) for u in range(2) for g in (2 * c, 2 * c + 1) if g < G]
N_PV = len(STEPS)
LAST_SUM = 2 * TILES
PAIR_AT = [0, 1, 2, 3, 4, 5, 6, 7]
LAST_AT = [3, 4, 5, 6]
QUERIES_AT = [0, 2, 4]
VALUES_AT = [1, 3, 5, 9]
PROJECT_AT = [0, 1, 2, 3]
G_AT, L_AT, PT_AT, SEM_AT, LN_AT = 7, 6, 8, 9, 8
BIAS_AT = [5, 6, 7, 8]
LH = P
N_ST = 2 * N_PV
NUMS_AT = [n for n, (g, u) in enumerate(STEPS) if g % 2 or g == G - 1]

C_ID = 0
C_COEF = C_ID + P
C_END = C_COEF + 4
B_ID = 0
B_SELT = B_ID + P
B_SELQ = B_SELT + TOK
B_END = B_SELQ + HG * N


def xattn_kernel(nc, xT, xr, ctxT, fside, wq, wk, wkip, wv, wout, bout, cf, cb, krows, out):
    ctx = ExitStack()
    with ctx:
        def sb(name, shape, dt):
            return ctx.enter_context(nc.sbuf_tensor(name, shape, dt))

        def sem(name):
            return ctx.enter_context(nc.semaphore(name))

        cfs = sb("cfs", [P, C_END], F32)
        cbs = sb("cbs", [P, B_END], BF16)
        wq_sb = sb("wq_sb", [P, 3, C], F32)
        wv_sb = sb("wv_sb", [P, KC, VW], F32)
        wout_sb = sb("wout_sb", [P, CHUNKS, C], F32)
        bias_sb = sb("bias_sb", [P, C], F32)
        mask_raw = sb("mask_raw", [P, S], F32)
        mask_sb = sb("mask_sb", [P, S], F32)
        ident = cfs[:, C_ID:C_ID + P]
        coef = cfs[:, C_COEF:C_END]
        ident_b = cbs[:, B_ID:B_ID + P]
        sel_t = cbs[:, B_SELT:B_SELT + TOK]
        sel_q = cbs[:, B_SELQ:B_END]
        weights_exps = sb("weights_exps", [P, 2 * KC * C], F32)
        wk_sb = weights_exps[:, 0:KC * C].rearrange("p (k n) -> p k n", k=KC)
        wkip_sb = weights_exps[:, KC * C:2 * KC * C].rearrange("p (k n) -> p k n", k=KC)
        row_exps = [weights_exps[:, 2 * HG * TOK * i:2 * HG * TOK * (i + 1)].rearrange("p (h t) -> p h t", t=TOK)
                    for i in range(2)]
        acc_exps = weights_exps[:, 4 * HG * TOK:5 * HG * TOK].rearrange("p (h t) -> p h t", t=TOK)
        ctx_hs_ob = sb("ctx_hs_ob", [P, 4 * KC * TOK2], F32)
        ctx_g = [ctx_hs_ob[:, 2 * KC * TOK2 * i:2 * KC * TOK2 * (i + 1)].rearrange("p (g k t) -> p g k t", g=2, k=KC)
                 for i in range(2)]
        hs = ctx_hs_ob[:, 0:CHUNKS * Q2].rearrange("p (g q) -> p g q", g=CHUNKS)
        ob = ctx_hs_ob[:, CHUNKS * Q2:CHUNKS * Q2 + TILES * C].rearrange("p (t n) -> p t n", t=TILES)
        rest = [sb(f"rest{i}", [P, Q2], F32) for i in range(2)]
        k_parts = sb("k_parts", [P, 3, 3, B * TOK], BF16)
        xT_sb = sb("xT_sb", [P, 3, Q2], F32)
        ctx_sb = [sb(f"ctx_sb{i}", [P, KC, TOK2], F32) for i in range(2)]
        xr_sb = sb("xr_sb", [P, TILES, C], F32)
        q_parts = sb("q_parts", [P, 3, 3, Q2], BF16)
        qpack = [sb(f"qpack{i}", [R_ALL, H, Q2], BF16) for i in range(2)]
        kpack = [sb(f"kpack{i}", [R_ALL, H, TOK2], BF16) for i in range(2)]
        v_sb = [[sb(f"v_sb{i}{u}", [TOK, 2, CHUNKS * HG, 32], F32) for u in range(2)] for i in range(2)]
        sempack = [sb(f"sempack{i}", [P, Q2], BF16) for i in range(2)]
        g_sb = [sb(f"g_sb{u}", [T, 3, N], F32) for u in range(2)]
        sem_low = sb("sem_low", [P, Q2], BF16)
        sem_hi = sb("sem_hi", [P, Q2], BF16)
        sem_mid = sem_hi
        sem_rest = sb("sem_rest", [P, Q2], F32)
        l_max = sb("l_max", [P, TILES], F32)
        l_den = sb("l_den", [P, TILES], F32)
        l_rec = sb("l_rec", [P, TILES], F32)
        l_exp = sb("l_exp", [P, TILES, T], F32)
        pT_sb = sb("pT_sb", [T, Q2], F32)
        m_neg = sb("m_neg", [P, 2, TILES * H], F32)
        z_sum = sb("z_sum", [P, 2, TILES * H], F32)
        z_ln = sb("z_ln", [P, 2, TILES * H], F32)
        m_rest = z_ln
        m_parts = sb("m_parts", [P, TILES, 3, 2, H], BF16)
        mT_sb = sb("mT_sb", [6 * H, Q2], BF16)
        pt = [sb(f"pt{i}", [TOK, HG, S], F32) for i in range(2)]

        def bank(name, banks=1):
            return ctx.enter_context(nc.psum_tensor(name, [P, 512 * banks], F32))

        PJ = [bank(f"PJ{i}") for i in range(2)]
        SQ2 = bank("SQ2", 2)
        SQ = [SQ2[:, 512 * i:512 * (i + 1)] for i in range(2)]
        LG = bank("LG")
        ST = [bank(f"ST{i}") for i in range(2)]
        NU = bank("NU")

        d_const, d_wk, d_w, d_ctx_g = sem("d_const"), sem("d_wk"), sem("d_w"), [sem("d_ctx_g0"), sem("d_ctx_g1")]
        d_xT, d_ctx, d_xr = sem("d_xT"), sem("d_ctx"), sem("d_xr")
        d_kpack = [sem(f"d_kpack{c}") for c in range(3)]
        d_qpack = [sem(f"d_qpack{c}") for c in range(3)]
        d_mrow, d_semrow, d_out = sem("d_mrow"), sem("d_semrow"), sem("d_out")
        k_mm, k_hi, k_rs, k_mid, k_low = (sem(n) for n in ("k_mm", "k_hi", "k_rs", "k_mid", "k_low"))
        q_mm, q_hi, q_rs, q_mid, q_low = (sem(n) for n in ("q_mm", "q_hi", "q_rs", "q_mid", "q_low"))
        v_mm, v_done, g_done = sem("v_mm"), sem("v_done"), sem("g_done")
        l_mm, l_maxed, l_exped, l_normed = sem("l_mm"), sem("l_maxed"), sem("l_exped"), sem("l_normed")
        l_recip = sem("l_recip")
        pT_mm, pT_done, sem_mm = sem("pT_mm"), sem("pT_done"), sem("sem_mm")
        s_hi, s_rest, s_mid, s_pack, s_low = (sem(n) for n in ("s_hi", "s_rest", "s_mid", "s_pack", "s_low"))
        sq_mm, sq_max, sq_sub, sq_exp = sem("sq_mm"), sem("sq_max"), sem("sq_sub"), sem("sq_exp")
        last_mm, last_max, g_mm = sem("last_mm"), sem("last_max"), sem("g_mm")
        sq_sum, sq_acc, ln_done = sem("sq_sum"), sem("sq_acc"), sem("ln_done")
        m_step, m_split, mT_mm, mT_done = sem("m_step"), sem("m_split"), sem("mT_mm"), sem("mT_done")
        st_mm, exped, masked, pv_mm, hs_done = sem("st_mm"), sem("exped"), sem("masked"), sem("pv_mm"), sem("hs_done")
        o_mm, o_done, xb_done = sem("o_mm"), sem("o_done"), sem("xb_done")
        mask_set, v_zero, v_half = sem("mask_set"), sem("v_zero"), sem("v_half")

        D_PACK = 16 * SLOTS
        ST_OF = [min(2 * 2 * 2 * (c + 1), N_ST) for c in range(3)]

        block = ctx.enter_context(nc.Block())

        def need(eng, s, value):
            if isinstance(value, int) and value <= 0:
                return
            eng.wait_ge(s, value)

        def run(eng, iteration):
            iteration(-1, 1, False, False, False, True)
            iteration(0, 0, False, False, True, True)
            iteration(1, 1, False, True, True, True)
            with eng.Fori(0, PAIRS // 2 - 2) as i:
                iteration(2 * i + 2, 0, True, True, True, True)
                iteration(2 * i + 3, 1, True, True, True, True)
            iteration(PAIRS - 2, 0, True, True, True, True)
            iteration(PAIRS - 1, 1, True, True, True, False)
            iteration(PAIRS, 0, True, True, False, False)
            iteration(PAIRS + 1, 1, True, False, False, False)

        @block.sync
        def _(sp):
            for k in range(KC):
                sp.dma_start(wk_sb[:, k, :], wk[k]).then_inc(d_wk, 16)
            sp.dma_start(ctx_g[0], ctxT[0:2].rearrange("g p k t -> p g k t")).then_inc(d_ctx_g[0], 16)
            for k in range(KC):
                sp.dma_start(wkip_sb[:, k, :], wkip[k]).then_inc(d_wk, 16)
            sp.dma_start(ctx_g[1], ctxT[2:4].rearrange("g p k t -> p g k t")).then_inc(d_ctx_g[1], 16)
            sp.dma_start(cfs[:], cf).then_inc(d_const, 16)
            sp.dma_start(cbs[:].bitcast(U16), cb).then_inc(d_const, 16)
            for i in range(2):
                sp.dma_start(kpack[i][R_SEM:R_ALL, :, :].bitcast(U16), krows).then_inc(d_const, 16)
            sp.dma_start(mask_raw[:], fside.rearrange("(a s) -> a s", a=1).broadcast_to((P, S))).then_inc(d_const, 16)
            sp.dma_start(bias_sb[:], bout.rearrange("(a s) -> a s", a=1).broadcast_to((P, C))).then_inc(d_const, 16)
            sp.dma_start(wq_sb[:], wq.rearrange("(c p) n -> p c n", p=P)).then_inc(d_w, 16)
            for k in range(KC):
                sp.dma_start(wv_sb[:, k, :], wv[k]).then_inc(d_w, 16)
            sp.dma_start(wout_sb[:], wout.rearrange("g p n -> p g n")).then_inc(d_w, 16)
            for g in range(2, GROUPS):
                sp.wait_ge(k_mm, 3 * (g - 1))
                sp.dma_start(ctx_g[g % 2], ctxT[2 * g:2 * g + 2].rearrange("g p k t -> p g k t")).then_inc(
                    d_ctx_g[g % 2], 16)

            def pack(j, q, c):
                nh = CH[c][1]
                for s in range(SLOTS):
                    sp.dma_start(kpack[q ^ 1][D * s:D * (s + 1), 8 * c:8 * c + nh, :],
                                 k_parts[0:D * nh, c, K_PART[s], bass.ds(TOK2 * (j + 1), TOK2)]).then_inc(d_kpack[c], 16)
                need(sp, q_low, 3 * (j + 1) + c + 1)
                for s in range(SLOTS):
                    sp.dma_start(qpack[q ^ 1][D * s:D * (s + 1), 8 * c:8 * c + nh, :],
                                 q_parts[0:D * nh, c, Q_PART[s], :]).then_inc(d_qpack[c], 16)

            def iteration(j, q, fin, old, cur, nxt):
                more = nxt and (not isinstance(j, int) or j + 2 < PAIRS)
                if not old and not cur and nxt:
                    sp.dma_start(xT_sb[:], xT[0].rearrange("c p q -> p c q")).then_inc(d_xT, 16)
                    for i in range(2):
                        sp.dma_start(ctx_sb[i][:], ctxT[i]).then_inc(d_ctx, 16)
                    sp.wait_ge(k_low, 3 * GROUPS)
                if fin:
                    need(sp, o_done, TILES * (j - 1))
                    sp.dma_start(out[j - 2], ob).then_inc(d_out, 16)
                if old:
                    sp.dma_start(xr_sb[:], xr[j - 1]).then_inc(d_xr, 16)
                if nxt:
                    for c in range(3):
                        if c == 2:
                            if more:
                                need(sp, q_mm, 3 * (j + 2))
                                sp.dma_start(xT_sb[:], xT[j + 2].rearrange("c p q -> p c q")).then_inc(d_xT, 16)
                            if cur:
                                need(sp, mT_done, j + 1)
                                sp.dma_start(qpack[q][R_MAX:R_ALL, :, :], mT_sb[:, :]).then_inc(d_mrow, 16)
                        if old:
                            sp.wait_ge(st_mm, N_ST * (j - 1) + ST_OF[c])
                        elif cur:
                            sp.wait_ge(last_mm if c == 2 else sq_mm, 1 if c == 2 else 2)
                        pack(j, q, c)
                elif cur:
                    need(sp, mT_done, j + 1)
                    sp.dma_start(qpack[q][R_MAX:R_ALL, :, :], mT_sb[:, :]).then_inc(d_mrow, 16)
                if cur and more:
                    need(sp, v_mm, 4 * (j + 1))
                    sp.dma_start(ctx_sb[q][:], ctxT[j + 2]).then_inc(d_ctx, 16)
                if nxt:
                    need(sp, s_low, j + 2)
                    sp.dma_start(qpack[q ^ 1][R_SEM:R_SEM + 1, :, :],
                                 sem_low[2 * N - 1:2 * N, :].unsqueeze(1).broadcast_to((1, H, Q2))).then_inc(
                                     d_semrow, 16)

            run(sp, iteration)
            sp.wait_ge(d_out, 16 * PAIRS)

        @block.tensor
        def _(pe):
            def key_group(g, i):
                pe.wait_ge(d_ctx_g[i], 16 * (g // 2 + 1) if isinstance(g, int) else 8 * (g - i) + 16)
                for c, nh in CH:
                    nr = D * nh
                    b = PJ[(3 * i + c) % 2]
                    if not (isinstance(g, int) and 3 * g + c - 1 <= 0):
                        pe.wait_ge(k_rs, 3 * g + c - 1)
                    ps = b[0:nr, 0:GB * TOK].rearrange("p (g b t) -> p g b t", g=2, b=2)
                    cg = ctx_g[i].rearrange("p g k (b t) -> p g k b t", b=2)
                    for w, t0, t1 in ((wk_sb, 0, T), (wkip_sb, T, TOK)):
                        for k in range(KC):
                            mm = pe.matmul(ps[:, :, :, t0:t1], w[:, k, P * c:P * c + nr], cg[:, :, k, :, t0:t1],
                                           start=(k == 0), stop=(k == KC - 1), skip_group_check=True)
                    mm.then_inc(k_mm, 1)

            pe.wait_ge(d_wk, 16 * 2 * KC)
            for g in range(GROUPS):
                key_group(g, g % 2)

            def queries(j, c):
                nr = ROWS[c]
                if c == 0:
                    pe.wait_ge(d_xT, 16 * (j + 2))
                    need(pe, v_done, 4 * j)
                else:
                    need(pe, q_rs, 3 * (j + 1) + c)
                for k in range(3):
                    mm = pe.matmul(PJ[1][0:nr, :], wq_sb[:, k, P * c:P * c + nr], xT_sb[:, k, :],
                                   start=(k == 0), stop=(k == 2))
                mm.then_inc(q_mm, 1)

            def values(j, q, i, nxt):
                u, half = divmod(i, 2)
                if i == 0:
                    need(pe, s_rest, j + 1)
                elif i < 3:
                    need(pe, v_done, 4 * j + i)
                elif nxt:
                    need(pe, pT_done, j + 2)
                else:
                    need(pe, v_done, 4 * j)
                b = PJ[1 if i == 3 else 0]
                for k in range(KC):
                    mm = pe.matmul(b[0:TOK, 0:VH[half]], ctx_sb[q][:, k, TOK * u:TOK * (u + 1)],
                                   wv_sb[:, k, VH[0] * half:VH[0] + VH[1] * half], start=(k == 0), stop=(k == KC - 1))
                mm.then_inc(v_mm, 1)

            def token_products(j, q):
                pe.wait_ge(d_ctx, 16 * min(j + 3, PAIRS) if isinstance(j, int) and j < 0 else 16 * (j + 2))
                need(pe, q_rs, 3 * (j + 2))
                for u in range(2):
                    for k in range(KC):
                        mm = pe.matmul(PJ[1][0:T, N * u:N * (u + 1)], ctx_sb[q ^ 1][:, k, TOK * u:TOK * u + T],
                                       ctx_sb[q ^ 1][:, k, TOK * u + T:TOK * (u + 1)], start=(k == 0),
                                       stop=(k == KC - 1), skip_group_check=True)
                mm.then_inc(g_mm, 1)

            def text_logits(j, cur):
                if cur:
                    need(pe, v_done, 4 * j + 3)
                need(pe, s_rest, j + 1)
                for c in range(3):
                    nr = ROWS[c]
                    need(pe, q_low, 3 * (j + 1) + c + 1)
                    for t in range(TILES):
                        for a, b in zip(Q_PART, K_PART):
                            mm = pe.matmul(PJ[0][:, T * t:T * (t + 1)], q_parts[0:nr, c, a, P * t:P * (t + 1)],
                                           k_parts[0:nr, c, b, bass.ds(TOK2 * (j + 1) + TOK * (t // 2), T)],
                                           start=(t == 0 and c == 0 and a + b == 0),
                                           stop=(c == 2 and a == 2), skip_group_check=True)
                mm.then_inc(l_mm, 1)

            def text_probs_T(j):
                need(pe, l_normed, j + 2)
                need(pe, g_done, 2 * (j + 2))
                for t in range(TILES):
                    mm = pe.transpose(PJ[1][0:T, P * t:P * (t + 1)], l_exp[:, t, :], ident)
                mm.then_inc(pT_mm, 1)

            def semantic(j):
                need(pe, pT_done, j + 2)
                need(pe, l_exped, TILES * (j + 2))
                for u in range(2):
                    mm = pe.matmul(PJ[0][:, S * u:S * (u + 1)], g_sb[u][:].rearrange("p r n -> p (r n)")[:, 0:P],
                                   pT_sb[:, S * u:S * (u + 1)], start=True, stop=True, skip_group_check=True)
                mm.then_inc(sem_mm, 1)

            def logits(j, q, t, g, b):
                for i in range(HG):
                    pe.matmul(b[:, LH * i:LH * i + TOK], qpack[q][0:R_QK, HG * g + i, P * t:P * (t + 1)],
                              kpack[q][0:R_QK, HG * g + i, TOK * (t // 2):TOK * (t // 2 + 1)],
                              start=(i == 0), stop=False, skip_group_check=True)
                ip = b[:, :].rearrange("p (h t) -> p h t", t=LH)[:, :, T:TOK]
                return pe.matmul(ip, sempack[q][:, P * t:P * (t + 1)], sel_q.rearrange("p (h n) -> p h n", h=HG),
                                 start=False, stop=True, skip_group_check=True)

            def rows(j, q, r):
                t, k = divmod(r, 2)
                if r == 0:
                    need(pe, s_pack, j + 1)
                    need(pe, mT_done, j)
                if t == 0:
                    pe.wait_ge(d_kpack[k], D_PACK * (j + 1))
                    pe.wait_ge(d_qpack[k], D_PACK * (j + 1))
                need(pe, sq_sub, LAST_SUM * j + r)
                logits(j, q, t, 2 * k, SQ[0])
                logits(j, q, t, 2 * k + 1, SQ[1]).then_inc(sq_mm, 1)

            def last_rows(j, q, t, fin):
                if t == 0:
                    pe.wait_ge(d_kpack[2], D_PACK * (j + 1))
                    pe.wait_ge(d_qpack[2], D_PACK * (j + 1))
                if fin and LAST_AT[t] <= PROJECT_AT[-1] + 1:
                    need(pe, o_done, TILES * (j - 2) + sum(p <= LAST_AT[t] for p in PROJECT_AT))
                need(pe, sq_acc, TILES * j + t)
                logits(j, q, t, G - 1, LG).then_inc(last_mm, 1)

            def maxima_T(j):
                need(pe, m_split, j + 1)
                need(pe, sq_sub, LAST_SUM * (j + 1))
                for t in range(TILES):
                    mm = pe.transpose(SQ[0].bitcast(BF16)[0:6 * H, P * t:P * (t + 1)],
                                      m_parts[:, t].rearrange("p a k h -> p (a k h)"), ident_b)
                mm.then_inc(mT_mm, 1)

            def columns(j, q, n):
                g, u = STEPS[n]
                if n == 0:
                    need(pe, d_mrow, 16 * j)
                    need(pe, d_semrow, 16 * j)
                for i in range(2):
                    need(pe, exped, N_ST * (j - 1) + 2 * n + i - 1)
                    pe.matmul(ST[i][0:TOK, :].rearrange("p (h q) -> p h q", h=2), sel_t,
                              sempack[q ^ 1][:, S * u:S * (u + 1)].unsqueeze(1).broadcast_to((P, 2, S)),
                              start=True, stop=False, skip_group_check=True)
                    for k in range(2):
                        h = HG * g + 2 * i + k
                        mm = pe.matmul(ST[i][0:TOK, S * k:S * (k + 1)], kpack[q ^ 1][:, h, TOK * u:TOK * (u + 1)],
                                       qpack[q ^ 1][:, h, S * u:S * (u + 1)],
                                       start=False, stop=(k == 1), skip_group_check=True)
                    mm.then_inc(st_mm, 1)

            def value_products(j, q, n):
                g, u = STEPS[n]
                c, e = divmod(g, 2)
                need(pe, masked, N_PV * (j - 1) + n + 1)
                if e == 0:
                    need(pe, hs_done, 2 * CHUNKS * (j - 1) + 2 * c + u)
                for i in range(HG):
                    mm = pe.matmul(NU[32 * i:32 * (i + 1), 0:S], v_sb[q ^ 1][u][:, e, HG * c + i, :], pt[n % 2][:, i, :],
                                   start=(e == 0), stop=(n in NUMS_AT), skip_group_check=True)
                mm.then_inc(pv_mm, 1)

            def project(j, t, cur):
                if t == 0:
                    need(pe, hs_done, 2 * CHUNKS * (j - 1))
                    if not isinstance(j, int) or j <= PAIRS:
                        need(pe, sq_acc, TILES * j)
                need(pe, o_done, TILES * (j - 2) + t)
                if cur:
                    need(pe, sq_acc, TILES * j + sum(s < PROJECT_AT[t] for s in LAST_AT))
                for c in range(CHUNKS):
                    mm = pe.matmul(LG[:, 0:C], hs[:, c, P * t:P * (t + 1)], wout_sb[:, c, :],
                                   start=(c == 0), stop=(c == CHUNKS - 1))
                mm.then_inc(o_mm, 1)

            pe.wait_ge(d_const, 16 * 6)
            pe.wait_ge(d_w, 16 * (2 + KC))
            pe.wait_ge(k_rs, 3 * GROUPS)

            def iteration(j, q, fin, old, cur, nxt):
                for n in range(N_PV):
                    if nxt and n == QUERIES_AT[0]:
                        queries(j, 0)
                    if cur and n in PAIR_AT:
                        rows(j, q, PAIR_AT.index(n))
                    if fin and n == PROJECT_AT[0]:
                        project(j, 0, cur)
                    if old:
                        columns(j, q, n)
                    if fin and n in PROJECT_AT[1:]:
                        project(j, PROJECT_AT.index(n), cur)
                    if nxt and n == SEM_AT:
                        semantic(j)
                    if old and n == N_PV - 1:
                        value_products(j, q, n - 1)
                    if cur and n in VALUES_AT:
                        values(j, q, VALUES_AT.index(n), nxt)
                    if nxt and n in QUERIES_AT[1:]:
                        queries(j, QUERIES_AT.index(n))
                    if nxt and n == G_AT:
                        token_products(j, q)
                    if nxt and n == L_AT:
                        text_logits(j, cur)
                    if nxt and n == PT_AT:
                        text_probs_T(j)
                    if old and 0 < n < N_PV - 1:
                        value_products(j, q, n - 1)
                    if cur and n in LAST_AT:
                        last_rows(j, q, LAST_AT.index(n), fin)
                if old:
                    value_products(j, q, N_PV - 1)
                if cur:
                    maxima_T(j)

            run(pe, iteration)

        @block.scalar
        def _(act):
            act.preload_act_table_set("natural_log_exp_and_others")
            for g in range(GROUPS):
                for c, nh in CH:
                    nr, n = D * nh, 3 * g + c
                    act.wait_ge(k_mm, n + 1)
                    act.activation(k_parts[0:nr, c, 0, GB * TOK * g:GB * TOK * (g + 1)], PJ[n % 2][0:nr, 0:GB * TOK],
                                   ACT.Copy).then_inc(k_hi, 1)
                    act.wait_ge(k_rs, n + 1)
                    act.activation(k_parts[0:nr, c, 1, GB * TOK * g:GB * TOK * (g + 1)], rest[n % 2][0:nr, 0:GB * TOK],
                                   ACT.Copy).then_inc(k_mid, 1)

            def q_high(j, c):
                nr = ROWS[c]
                need(act, q_mm, 3 * (j + 1) + c + 1)
                need(act, d_qpack[c], D_PACK * (j + 1))
                need(act, l_mm, j + 1)
                act.activation(q_parts[0:nr, c, 0, :], PJ[1][0:nr, :], ACT.Copy, scale=SCALE).then_inc(q_hi, 1)

            def q_middle(j, c):
                nr = ROWS[c]
                need(act, q_rs, 3 * (j + 1) + c + 1)
                act.activation(q_parts[0:nr, c, 1, :], rest[c % 2][0:nr, :], ACT.Copy).then_inc(q_mid, 1)

            def softmax_exp(j, n):
                if n >= 2:
                    need(act, pv_mm, N_PV * (j - 1) + n - 1)
                for i in range(2):
                    need(act, st_mm, N_ST * (j - 1) + 2 * n + i + 1)
                    act.activation(pt[n % 2][:, 2 * i:2 * i + 2, :].rearrange("p h q -> p (h q)"), ST[i][0:TOK, :],
                                   ACT.Exp).then_inc(exped, 1)

            def row_exp(j, r):
                need(act, sq_sub, LAST_SUM * j + r + 1)
                act.activation(row_exps[r % 2][:, :, :], row_exps[r % 2][:, :, :], ACT.Exp).then_inc(sq_exp, 1)

            def last_exp(j, t):
                need(act, last_max, TILES * j + t + 1)
                need(act, sq_acc, TILES * j + t)
                for i in range(HG):
                    for kind, t0, t1 in ((0, 0, T), (1, T, TOK)):
                        at = H * t + HG * (G - 1) + i
                        done = act.activation(acc_exps[:, i, t0:t1], LG[:, LH * i + t0:LH * i + t1], ACT.Exp,
                                              bias=m_neg[:, kind, at:at + 1], accum_out=z_sum[:, kind, at:at + 1])
                done.then_inc(sq_acc, 1)

            def products_out(j, n):
                g, u = STEPS[n]
                need(act, pv_mm, N_PV * (j - 1) + n + 1)
                if n == NUMS_AT[0]:
                    need(act, o_mm, TILES * (j - 2) + 2)
                if n == NUMS_AT[1]:
                    need(act, o_mm, TILES * (j - 1))
                act.activation(hs[:, g // 2, S * u:S * (u + 1)], NU[:, 0:S], ACT.Copy).then_inc(hs_done, 1)

            def g_out(j, u):
                need(act, g_mm, j + 2)
                need(act, sem_mm, j + 1)
                act.activation(g_sb[u][:], PJ[1][0:T, N * u:N * (u + 1)].unsqueeze(1).broadcast_to((T, 3, N)), ACT.Copy,
                               scale=SCALE * SEM_SCALE).then_inc(g_done, 1)

            def iteration(j, q, fin, old, cur, nxt):
                for n in range(N_PV):
                    if nxt and n == QUERIES_AT[0]:
                        q_high(j, 0)
                    if old and n - 2 in NUMS_AT:
                        products_out(j, n - 2)
                    if cur and n - 1 in LAST_AT:
                        last_exp(j, LAST_AT.index(n - 1))
                    if old:
                        softmax_exp(j, n)
                    if nxt and n - 1 in QUERIES_AT:
                        q_middle(j, QUERIES_AT.index(n - 1))
                    if nxt and n == L_AT + 1:
                        need(act, l_maxed, j + 2)
                        need(act, l_normed, j + 1)
                        for t in range(TILES):
                            act.activation(l_exp[:, t, :], PJ[0][:, T * t:T * (t + 1)], ACT.Exp, bias=l_max[:, t:t + 1],
                                           accum_out=l_den[:, t:t + 1]).then_inc(l_exped, 1)
                    if nxt and n == G_AT:
                        g_out(j, 0)
                        g_out(j, 1)
                    if cur and n in PAIR_AT:
                        row_exp(j, PAIR_AT.index(n))
                    if nxt and n in QUERIES_AT[1:]:
                        q_high(j, QUERIES_AT.index(n))
                    if nxt and n == PT_AT:
                        need(act, pT_mm, j + 2)
                        need(act, sem_mm, j + 1)
                        act.activation(pT_sb[:, :], PJ[1][0:T, :], ACT.Copy).then_inc(pT_done, 1)
                    if cur and n == LN_AT:
                        need(act, sq_sum, LAST_SUM * (j + 1))
                        need(act, sq_acc, TILES * (j + 1))
                        need(act, m_split, j)
                        act.activation(z_ln[:, :, :], z_sum[:, :, :], ACT.Ln).then_inc(ln_done, 1)
                    if nxt and n == SEM_AT:
                        need(act, sem_mm, j + 2)
                        need(act, s_pack, j + 1)
                        need(act, s_low, j + 1)
                        act.activation(sem_hi[:, :], PJ[0][:, :], ACT.Copy).then_inc(s_hi, 1)
                    if old and n == N_PV - 1:
                        products_out(j, n - 1)
                    if nxt and n == SEM_AT:
                        need(act, s_rest, j + 2)
                        act.activation(sem_mid[:, :], sem_rest[:, :], ACT.Copy).then_inc(s_mid, 1)
                if old:
                    products_out(j, N_PV - 1)
                if cur:
                    need(act, mT_mm, j + 1)
                    need(act, d_mrow, 16 * j)
                    act.activation(mT_sb[:, :], SQ[0].bitcast(BF16)[0:6 * H, 0:Q2], ACT.Copy).then_inc(mT_done, 1)

            run(act, iteration)

        @block.vector
        def _(dve):
            dve.wait_ge(d_const, 16 * 6)
            dve.tensor_scalar(mask_sb[:, :], mask_raw[:, :], coef[:, 3:4], coef[:, 2:3], ALU.mult,
                              ALU.add).then_inc(mask_set, 1)
            for g in range(GROUPS):
                for c, nh in CH:
                    nr, n = D * nh, 3 * g + c
                    dve.wait_ge(k_hi, n + 1)
                    need(dve, k_low, n - 1)
                    dve.tensor_tensor(rest[n % 2][0:nr, 0:GB * TOK], PJ[n % 2][0:nr, 0:GB * TOK],
                                      k_parts[0:nr, c, 0, GB * TOK * g:GB * TOK * (g + 1)],
                                      ALU.subtract).then_inc(k_rs, 1)

            def heads(t, g0, g1):
                return slice(H * t + HG * g0, H * t + HG * g1)

            def maxima(b, at, done):
                b = b[:, :].rearrange("p (h t) -> p h t", t=LH)
                dve.tensor_reduce(m_neg[:, 0, at], b[:, :, 0:T], AX_X, ALU.max, negate=True)
                dve.tensor_reduce(m_neg[:, 1, at], b[:, :, T:TOK], AX_X, ALU.max, negate=True).then_inc(done, 1)

            def row_max(j, r):
                t, k = divmod(r, 2)
                need(dve, sq_mm, LAST_SUM * j + r + 1)
                if r == 0:
                    need(dve, m_split, j)
                at = heads(t, 2 * k, 2 * k + 2)
                maxima(SQ2, at, sq_max)
                need(dve, sq_max, LAST_SUM * j + r + 1)
                if r >= 2:
                    need(dve, sq_sum, LAST_SUM * j + r - 1)
                b = SQ2[:, :].rearrange("p (h t) -> p h t", t=LH)
                for kind, t0, t1 in ((0, 0, T), (1, T, TOK)):
                    done = dve.tensor_tensor(row_exps[r % 2][:, :, t0:t1], b[:, :, t0:t1],
                                             m_neg[:, kind, at].unsqueeze(2).broadcast_to((P, 2 * HG, t1 - t0)), ALU.add)
                done.then_inc(sq_sub, 1)

            def last_row_max(j, t):
                need(dve, last_mm, TILES * j + t + 1)
                maxima(LG, heads(t, G - 1, G), last_max)

            def row_sum(j, r):
                t, k = divmod(r, 2)
                need(dve, sq_exp, LAST_SUM * j + r + 1)
                if r == 0:
                    need(dve, ln_done, j)
                at = heads(t, 2 * k, 2 * k + 2)
                dve.tensor_reduce(z_sum[:, 0, at], row_exps[r % 2][:, :, 0:T], AX_X, ALU.add)
                dve.tensor_reduce(z_sum[:, 1, at], row_exps[r % 2][:, :, T:TOK], AX_X, ALU.add).then_inc(sq_sum, 1)

            def split_maxima(j):
                def by_tile(a):
                    return a[:, :, :].rearrange("p k (t h) -> p t k h", t=TILES)
                need(dve, ln_done, j + 1)
                need(dve, mT_mm, j)
                dve.tensor_tensor(m_neg[:, :, :], m_neg[:, :, :], z_ln[:, :, :], ALU.subtract).then_inc(m_step, 1)
                need(dve, m_step, 4 * j + 1)
                dve.tensor_copy(m_parts[:, :, 0], by_tile(m_neg)).then_inc(m_step, 1)
                need(dve, m_step, 4 * j + 2)
                dve.tensor_tensor(by_tile(m_rest), by_tile(m_neg), m_parts[:, :, 0], ALU.subtract).then_inc(m_step, 1)
                need(dve, m_step, 4 * j + 3)
                dve.tensor_copy(m_parts[:, :, 1], by_tile(m_rest)).then_inc(m_step, 1)
                need(dve, m_step, 4 * j + 4)
                dve.tensor_tensor(m_parts[:, :, 2], by_tile(m_rest), m_parts[:, :, 1], ALU.subtract).then_inc(m_split, 1)

            def q_remainder(j, c):
                nr = ROWS[c]
                need(dve, q_hi, 3 * (j + 1) + c + 1)
                need(dve, q_low, 3 * (j + 1) + c - 1)
                dve.scalar_tensor_tensor(rest[c % 2][0:nr, :], PJ[1][0:nr, :], SCALE, q_parts[0:nr, c, 0, :],
                                         ALU.mult, ALU.subtract).then_inc(q_rs, 1)

            def values_out(j, q, i):
                u, half = divmod(i, 2)
                v = v_sb[q][u][:, half, 0:HG * VG[half], D * half:D * (half + 1)]
                b = PJ[1 if i == 3 else 0][0:TOK, 0:VH[half]].rearrange("p (h k d) -> p h k d", k=2, d=D)
                if i == 0:
                    need(dve, pv_mm, N_PV * (j - 1))
                need(dve, v_mm, 4 * j + i + 1)
                dve.tensor_scalar(v, b[:, :, 0, :], coef[0:TOK, 2:3], None, ALU.mult).then_inc(v_half, 1)
                need(dve, v_half, 4 * j + i + 1)
                dve.scalar_tensor_tensor(v, b[:, :, 1, :], coef[0:TOK, 3:4], v, ALU.mult, ALU.add).then_inc(v_done, 1)

            def output(j, t):
                if t == 0:
                    need(dve, d_out, 16 * (j - 2))
                    need(dve, xb_done, TILES * (j - 1))
                need(dve, o_mm, TILES * (j - 2) + t + 1)
                dve.tensor_tensor(ob[:, t, :], LG[:, 0:C], xr_sb[:, t, :], ALU.add).then_inc(o_done, 1)

            def iteration(j, q, fin, old, cur, nxt):
                for n in range(N_PV):
                    if cur and n - 1 in PAIR_AT:
                        row_sum(j, PAIR_AT.index(n - 1))
                    if nxt and n - 1 in QUERIES_AT:
                        q_remainder(j, QUERIES_AT.index(n - 1))
                    if nxt and n == L_AT + 1:
                        need(dve, l_mm, j + 2)
                        dve.tensor_reduce(l_max[:, :], PJ[0][:, 0:TILES * T].rearrange("p (t k) -> p t k", t=TILES), AX_X,
                                          ALU.max, negate=True).then_inc(l_maxed, 1)
                    if cur and n in PAIR_AT:
                        row_max(j, PAIR_AT.index(n))
                    if fin and n in PROJECT_AT:
                        output(j, PROJECT_AT.index(n))
                    if nxt and n == L_AT + 1:
                        need(dve, l_exped, TILES * (j + 2))
                        dve.reciprocal(l_rec[:, :], l_den[:, :]).then_inc(l_recip, 1)
                        need(dve, l_recip, j + 2)
                        need(dve, pT_mm, j + 1)
                        dve.tensor_tensor(l_exp[:, :, :], l_exp[:, :, :],
                                          l_rec[:, :].unsqueeze(2).broadcast_to((P, TILES, T)), ALU.mult).then_inc(
                                              l_normed, 1)
                    if cur and n == LN_AT + 1:
                        split_maxima(j)
                    if nxt and n == SEM_AT:
                        need(dve, s_hi, j + 2)
                        need(dve, s_pack, j + 1)
                        need(dve, s_low, j + 1)
                        dve.scalar_tensor_tensor(sem_rest[:, :], sem_hi[:, :], coef[:, 0:1], PJ[0][:, :], ALU.mult,
                                                 ALU.add).then_inc(s_rest, 1)
                        need(dve, s_mid, j + 2)
                        need(dve, s_rest, j + 2)
                        if old:
                            need(dve, st_mm, N_ST * j)
                        dve.scalar_tensor_tensor(sempack[q ^ 1][:, :], sem_mid[:, :], coef[:, 1:2], sem_rest[:, :],
                                                 ALU.mult, ALU.add).then_inc(s_pack, 1)
                    if cur and n in VALUES_AT:
                        values_out(j, q, VALUES_AT.index(n))
                    if cur and n in LAST_AT:
                        last_row_max(j, LAST_AT.index(n))

            dve.wait_ge(k_low, 3 * GROUPS)
            dve.wait_ge(v_zero, 4)
            run(dve, iteration)

        @block.gpsimd
        def _(pool):
            for i in range(2):
                for u in range(2):
                    pool.memset(v_sb[i][u][:], 0.0).then_inc(v_zero, 1)
            for g in range(GROUPS):
                for c, nh in CH:
                    nr, n = D * nh, 3 * g + c
                    pool.wait_ge(k_mid, n + 1)
                    pool.tensor_tensor(k_parts[0:nr, c, 2, GB * TOK * g:GB * TOK * (g + 1)], rest[n % 2][0:nr, 0:GB * TOK],
                                       k_parts[0:nr, c, 1, GB * TOK * g:GB * TOK * (g + 1)],
                                       ALU.subtract).then_inc(k_low, 1)
            pool.wait_ge(d_const, 16 * 6)
            pool.wait_ge(mask_set, 1)

            def mask_probs(j, n):
                need(pool, exped, N_ST * (j - 1) + 2 * n + 2)
                pool.tensor_tensor(pt[n % 2][:, :, :], pt[n % 2][:, :, :],
                                   mask_sb[0:TOK, :].unsqueeze(1).broadcast_to((TOK, HG, S)), ALU.mult).then_inc(masked, 1)

            def iteration(j, q, fin, old, cur, nxt):
                for n in range(N_PV):
                    if old:
                        mask_probs(j, n)
                    if nxt and n - 1 in QUERIES_AT:
                        c = QUERIES_AT.index(n - 1)
                        nr = ROWS[c]
                        need(pool, q_mid, 3 * (j + 1) + c + 1)
                        pool.tensor_tensor(q_parts[0:nr, c, 2, :], rest[c % 2][0:nr, :], q_parts[0:nr, c, 1, :],
                                           ALU.subtract).then_inc(q_low, 1)
                    if old and n in BIAS_AT:
                        t = BIAS_AT.index(n)
                        need(pool, d_xr, 16 * j)
                        pool.tensor_tensor(xr_sb[:, t, :], xr_sb[:, t, :], bias_sb[:, :], ALU.add).then_inc(xb_done, 1)
                if nxt:
                    need(pool, s_mid, j + 2)
                    need(pool, d_semrow, 16 * (j + 1))
                    pool.tensor_tensor(sem_low[:, :], sem_rest[:, :], sem_mid[:, :], ALU.subtract).then_inc(s_low, 1)
            run(pool, iteration)


def constants():
    import numpy as np

    f = np.zeros((P, C_END), np.float32)
    f[:, C_ID:C_ID + P] = np.eye(P)
    f[N:, C_COEF] = -1.0
    f[2 * N:, C_COEF + 1] = -1.0
    f[0:T, C_COEF + 2] = 1.0
    f[T:, C_COEF + 3] = 1.0

    b = np.zeros((P, B_END), np.float32)
    b[:, B_ID:B_ID + P] = np.eye(P)
    for r in range(P):
        b[r, B_SELT + T + r % N] = 1.0
        for i in range(HG):
            b[r, B_SELQ + N * i + r % N] = 1.0
    k = np.zeros((R_ALL - R_SEM, H, 2, TOK), np.float32)
    k[0, :, :, TOK - 1] = 1.0
    for part in range(3):
        k[1 + 2 * part, :, :, 0:T] = 1.0
        k[2 + 2 * part, :, :, T:TOK] = 1.0
    return f, (b.view(np.uint32) >> 16).astype(np.uint16), (
        k.reshape(-1, H, TOK2).view(np.uint32) >> 16).astype(np.uint16)


def kernel(**inputs):
    import numpy as np
    import concourse.bacc as bacc
    from concourse.bass_utils import run_bass_kernel_spmd

    a = {k: np.asarray(v) for k, v in inputs.items()}

    def by_chunk(w):
        return np.concatenate([w[:, P * c:P * c + D * nh].reshape(-1, nh, D).transpose(0, 2, 1).reshape(-1, D * nh)
                               for c, nh in CH], 1)

    x = a["x"]
    xT = x.reshape(PAIRS, Q2, C).transpose(0, 2, 1)
    xT = np.pad(xT, ((0, 0), (0, 3 * P - C), (0, 0))).reshape(PAIRS, 3, P, Q2)
    xr = x.reshape(PAIRS, TILES, P, C).transpose(0, 2, 1, 3)
    ctxT = a["ctx_2048"].reshape(PAIRS, TOK2, KC, P).transpose(0, 3, 2, 1)
    wv = np.stack([a["L0_xattn_Wv"].reshape(CD, H, D), a["L0_xattn_Wv_ip"].reshape(CD, H, D)], 2)
    wv = wv.reshape(CD, G, HG * SEG)
    wv = np.concatenate([wv[:, 0::2], wv[:, 1::2]], 1)
    wo = np.pad(a["L0_xattn_Wout"].reshape(G, HG, D, C), ((0, 2 * CHUNKS - G), (0, 0), (0, 0), (0, 0)))
    wo = wo.reshape(CHUNKS, 2, HG, D, C).transpose(0, 2, 1, 3, 4).reshape(CHUNKS, P, C)
    f, b, k = constants()
    arrays = {
        "xT": xT, "xr": xr, "ctxT": ctxT, "fside": a["fside_S_0"],
        "wq": np.pad(by_chunk(a["L0_xattn_Wq"]), ((0, 3 * P - C), (0, 0))),
        "wk": by_chunk(a["L0_xattn_Wk"]).reshape(KC, P, C),
        "wkip": by_chunk(a["L0_xattn_Wk_ip"]).reshape(KC, P, C),
        "wv": wv.reshape(KC, P, VW), "wout": wo, "bout": a["L0_xattn_bout"],
        "cf": f, "cb": b, "krows": k,
    }
    arrays = {n: np.ascontiguousarray(v) for n, v in arrays.items()}
    nc = bacc.Bacc("TRN2", target_bir_lowering=False, num_devices=1)
    args = [nc.dram_tensor(n, v.shape, mybir.dt.from_np(v.dtype), kind="ExternalInput").ap()
            for n, v in arrays.items()]
    out = nc.dram_tensor("out", (PAIRS, P, TILES, C), F32, kind="ExternalOutput").ap()
    xattn_kernel(nc, *args, out)
    r = run_bass_kernel_spmd(nc, [arrays], core_ids=[0])
    return r.results[0]["out"].transpose(0, 2, 1, 3).reshape(B, S, C)
```

```python
from contextlib import ExitStack

import concourse.bass as bass
from concourse import mybir

F32 = mybir.dt.float32
BF16 = mybir.dt.bfloat16
U16 = mybir.dt.uint16
ALU = mybir.AluOpType
ACT = mybir.ActivationFunctionType
AX_X = mybir.AxisListType.X

B, S, C, CD = 16, 256, 320, 512
H = 20
D = C // H
T, N = 77, 43
TOK = T + N
P = 128
PAIRS = B // 2
Q2 = 2 * S
TOK2 = 2 * TOK
KC = CD // P
CH = [(0, 8), (1, 8), (2, 4)]
ROWS = [D * nh for _, nh in CH]
TILES = Q2 // P
HG = 4
G = H // HG
GB = 4
GROUPS = B // GB
SCALE = 1.0 / D ** 0.5
SEM_SCALE = 0.5
Q_PART = [0, 0, 0, 1, 1, 2]
K_PART = [0, 1, 2, 0, 1, 0]
SLOTS = len(Q_PART)
R_QK = SLOTS * D
R_SEM = R_QK
R_MAX = R_QK + 1
R_ALL = R_MAX + 6
VG = [(G + 1) // 2, G // 2]
IP0 = 2 * T
CHUNKS = VG[0]
STEPS = [(g, u) for c in range(CHUNKS) for u in range(2) for g in (2 * c, 2 * c + 1) if g < G]
N_PV = len(STEPS)
LAST_SUM = 2 * TILES
PAIR_AT = [0, 1, 2, 3, 4, 5, 6, 7]
LAST_AT = [2, 3, 4, 6]
QUERIES_AT = [0, 2, 4]
VALUES_AT = [1, 7, 9]
PROJECT_AT = [0, 1, 2, 3]
G_AT, L_AT, PT_AT, SEM_AT, LN_AT = 6, 6, 8, 9, 8
BIAS_AT = [5, 5, 6, 9]
START = "K K K Q0 K Q1 K Q2 G K K L K P K S K K K".split()
LH = P
N_ST = 2 * N_PV
NUMS_AT = [n for n, (g, u) in enumerate(STEPS) if g % 2 or g == G - 1]

C_ID = 0
C_COEF = C_ID + P
C_END = C_COEF + 4
B_ID = 0
B_SELT = B_ID + P
B_SELQ = B_SELT + TOK
B_END = B_SELQ + HG * N


def xattn_kernel(nc, xT, xr, ctxT, fside, wq, wk, wkip, wv, wout, bout, cf, cb, krows, out):
    ctx = ExitStack()
    with ctx:
        def sb(name, shape, dt):
            return ctx.enter_context(nc.sbuf_tensor(name, shape, dt))

        def sem(name):
            return ctx.enter_context(nc.semaphore(name))

        cfs = sb("cfs", [P, C_END], F32)
        cbs = sb("cbs", [P, B_END], BF16)
        wq_sb = sb("wq_sb", [P, 3, C], F32)
        wv_sb = sb("wv_sb", [P, KC, 2, C], F32)
        wout_sb = sb("wout_sb", [P, CHUNKS, C], F32)
        bias_sb = sb("bias_sb", [P, C], F32)
        mask_raw = sb("mask_raw", [P, S], F32)
        mask_sb = sb("mask_sb", [P, S], F32)
        ident = cfs[:, C_ID:C_ID + P]
        coef = cfs[:, C_COEF:C_END]
        ident_b = cbs[:, B_ID:B_ID + P]
        sel_t = cbs[:, B_SELT:B_SELT + TOK]
        sel_q = cbs[:, B_SELQ:B_END]
        weights_exps = sb("weights_exps", [P, 2 * KC * C], F32)
        wk_sb = weights_exps[:, 0:KC * C].rearrange("p (k n) -> p k n", k=KC)
        wkip_sb = weights_exps[:, KC * C:2 * KC * C].rearrange("p (k n) -> p k n", k=KC)
        row_exps = [weights_exps[:, 2 * HG * TOK * i:2 * HG * TOK * (i + 1)].rearrange("p (h t) -> p h t", t=TOK)
                    for i in range(2)]
        acc_exps = weights_exps[:, 4 * HG * TOK:5 * HG * TOK].rearrange("p (h t) -> p h t", t=TOK)
        ctx_hs_ob = sb("ctx_hs_ob", [P, 4 * KC * TOK2], F32)
        ctx_g = [ctx_hs_ob[:, 2 * KC * TOK2 * i:2 * KC * TOK2 * (i + 1)].rearrange("p (g k t) -> p g k t", g=2, k=KC)
                 for i in range(2)]
        hs = ctx_hs_ob[:, 0:CHUNKS * Q2].rearrange("p (g q) -> p g q", g=CHUNKS)
        ob = ctx_hs_ob[:, CHUNKS * Q2:CHUNKS * Q2 + TILES * C].rearrange("p (t n) -> p t n", t=TILES)
        v_ip = ctx_hs_ob[0:2 * N, CHUNKS * Q2 + TILES * C:CHUNKS * Q2 + TILES * C + 2 * CHUNKS * HG * 32].rearrange(
            "p (e h d) -> p e h d", e=2, d=32)
        rest = [sb(f"rest{i}", [P, Q2], F32) for i in range(2)]
        k_parts = sb("k_parts", [P, 3, 3, B * TOK], BF16)
        xT_sb = sb("xT_sb", [P, 3, Q2], F32)
        ctx_sb = [sb(f"ctx_sb{i}", [P, KC, TOK2], F32) for i in range(2)]
        xr_sb = sb("xr_sb", [P, TILES, C], F32)
        k_rest = [xr_sb[:, 2 * i:2 * i + 2, :].rearrange("p t n -> p (t n)") for i in range(2)]
        q_parts = sb("q_parts", [P, 3, 3, Q2], BF16)
        qpack = [sb(f"qpack{i}", [R_ALL, H, Q2], BF16) for i in range(2)]
        kpack = [sb(f"kpack{i}", [R_ALL, H, TOK2], BF16) for i in range(2)]
        v_sb = [[sb(f"v_sb{i}{u}", [TOK, 2, CHUNKS * HG, 32], F32) for u in range(2)] for i in range(2)]
        sempack = [sb(f"sempack{i}", [P, Q2], BF16) for i in range(2)]
        g_sb = [sb(f"g_sb{u}", [T, 3, N], F32) for u in range(2)]
        sem_low = sb("sem_low", [P, Q2], BF16)
        sem_hi = sb("sem_hi", [P, Q2], BF16)
        sem_mid = sem_hi
        sem_rest = sb("sem_rest", [P, Q2], F32)
        l_max = sb("l_max", [P, TILES], F32)
        l_den = sb("l_den", [P, TILES], F32)
        l_rec = sb("l_rec", [P, TILES], F32)
        l_exp = sb("l_exp", [P, TILES, T], F32)
        pT_sb = sb("pT_sb", [T, Q2], F32)
        m_neg = sb("m_neg", [P, 2, TILES * H], F32)
        z_sum = sb("z_sum", [P, 2, TILES * H], F32)
        z_ln = sb("z_ln", [P, 2, TILES * H], F32)
        m_rest = z_ln
        m_parts = sb("m_parts", [P, TILES, 3, 2, H], BF16)
        mT_sb = sb("mT_sb", [6 * H, Q2], BF16)
        pt = [sb(f"pt{i}", [TOK, HG, S], F32) for i in range(2)]

        def bank(name, banks=1):
            return ctx.enter_context(nc.psum_tensor(name, [P, 512 * banks], F32))

        PJ = [bank(f"PJ{i}") for i in range(2)]
        SQ2 = bank("SQ2", 2)
        SQ = [SQ2[:, 512 * i:512 * (i + 1)] for i in range(2)]
        LG = bank("LG")
        ST = [bank(f"ST{i}") for i in range(2)]
        NU = bank("NU")

        d_const, d_wk, d_wkip, d_wq, d_w, d_ctx_g = sem("d_const"), sem("d_wk"), sem("d_wkip"), sem("d_wq"), sem("d_w"), [sem("d_ctx_g0"), sem("d_ctx_g1")]
        d_xT, d_ctx, d_xr = sem("d_xT"), sem("d_ctx"), sem("d_xr")
        d_kpack = [sem(f"d_kpack{c}") for c in range(3)]
        d_qpack = [sem(f"d_qpack{c}") for c in range(3)]
        d_mrow, d_semrow, d_out = sem("d_mrow"), sem("d_semrow"), sem("d_out")
        k_mm, k_hi, k_rs, k_mid, k_low = (sem(n) for n in ("k_mm", "k_hi", "k_rs", "k_mid", "k_low"))
        q_mm, q_hi, q_rs, q_mid, q_low = (sem(n) for n in ("q_mm", "q_hi", "q_rs", "q_mid", "q_low"))
        v_mm, v_done, g_done = sem("v_mm"), sem("v_done"), sem("g_done")
        l_mm, l_maxed, l_exped, l_normed = sem("l_mm"), sem("l_maxed"), sem("l_exped"), sem("l_normed")
        l_recip = sem("l_recip")
        pT_mm, pT_done, sem_mm = sem("pT_mm"), sem("pT_done"), sem("sem_mm")
        s_hi, s_rest, s_mid, s_pack, s_low = (sem(n) for n in ("s_hi", "s_rest", "s_mid", "s_pack", "s_low"))
        sq_mm, sq_max, sq_sub, sq_exp = sem("sq_mm"), sem("sq_max"), sem("sq_sub"), sem("sq_exp")
        last_mm, last_max, g_mm = sem("last_mm"), sem("last_max"), sem("g_mm")
        sq_sum, sq_acc, ln_done = sem("sq_sum"), sem("sq_acc"), sem("ln_done")
        m_step, m_split, mT_mm, mT_done = sem("m_step"), sem("m_split"), sem("mT_mm"), sem("mT_done")
        st_mm, exped, masked, pv_mm, hs_done = sem("st_mm"), sem("exped"), sem("masked"), sem("pv_mm"), sem("hs_done")
        o_mm, o_done, xb_done = sem("o_mm"), sem("o_done"), sem("xb_done")
        mask_set, v_zero, d_v, parts_zero = (sem(n) for n in ("mask_set", "v_zero", "d_v", "parts_zero"))

        D_PACK = 16 * SLOTS
        ST_OF = [min(2 * 2 * 2 * (c + 1), N_ST) for c in range(3)]

        block = ctx.enter_context(nc.Block())

        def need(eng, s, value):
            if isinstance(value, int) and value <= 0:
                return
            eng.wait_ge(s, value)

        def output_bank(j, t):
            return ([LG, SQ[0], SQ[1], PJ[0]] if isinstance(j, int) and j == PAIRS + 1 else [LG, LG, PJ[0], PJ[0]])[t]

        def mask_on_vector(j):
            return isinstance(j, int) and j == PAIRS

        def mask_probs(eng, j, n):
            need(eng, exped, N_ST * (j - 1) + 2 * n + 2)
            eng.tensor_tensor(pt[n % 2][:, :, :], pt[n % 2][:, :, :],
                              mask_sb[0:TOK, :].unsqueeze(1).broadcast_to((TOK, HG, S)), ALU.mult).then_inc(masked, 1)

        def run(eng, iteration):
            iteration(0, 0, False, False, True, True)
            iteration(1, 1, False, True, True, True)
            with eng.Fori(0, PAIRS // 2 - 2) as i:
                iteration(2 * i + 2, 0, True, True, True, True)
                iteration(2 * i + 3, 1, True, True, True, True)
            iteration(PAIRS - 2, 0, True, True, True, True)
            iteration(PAIRS - 1, 1, True, True, True, False)
            iteration(PAIRS, 0, True, True, False, False)
            iteration(PAIRS + 1, 1, True, False, False, False)

        @block.sync
        def _(sp):
            sp.dma_start(ctx_g[0], ctxT[0:2].rearrange("g p k t -> p g k t")).then_inc(d_ctx_g[0], 16)
            for k in range(KC):
                sp.dma_start(wk_sb[:, k, :], wk[k]).then_inc(d_wk, 16)
            for k in range(KC):
                sp.dma_start(wkip_sb[:, k, :], wkip[k]).then_inc(d_wkip, 16)
            sp.dma_start(ctx_g[1], ctxT[2:4].rearrange("g p k t -> p g k t")).then_inc(d_ctx_g[1], 16)
            sp.dma_start(xT_sb[:], xT[0].rearrange("c p q -> p c q")).then_inc(d_xT, 16)
            sp.dma_start(wq_sb[:], wq.rearrange("(c p) n -> p c n", p=P)).then_inc(d_wq, 16)
            sp.dma_start(ctx_sb[0][:], ctxT[0]).then_inc(d_ctx, 16)
            sp.dma_start(cfs[:], cf).then_inc(d_const, 16)
            sp.dma_start(cbs[:].bitcast(U16), cb).then_inc(d_const, 16)
            for i in range(2):
                sp.dma_start(kpack[i][R_SEM:R_ALL, :, :].bitcast(U16), krows).then_inc(d_const, 16)
            sp.dma_start(mask_raw[:], fside.rearrange("(a s) -> a s", a=1).broadcast_to((P, S))).then_inc(d_const, 16)
            sp.dma_start(bias_sb[:], bout.rearrange("(a s) -> a s", a=1).broadcast_to((P, C))).then_inc(d_const, 16)
            sp.wait_ge(k_mm, 3)
            sp.dma_start(ctx_g[0], ctxT[4:6].rearrange("g p k t -> p g k t")).then_inc(d_ctx_g[0], 16)
            for k in range(KC):
                sp.dma_start(wv_sb[:, k, :], wv[k]).then_inc(d_w, 16)
            sp.dma_start(wout_sb[:], wout.rearrange("g p n -> p g n")).then_inc(d_w, 16)
            sp.wait_ge(k_low, 3)

            def pack(j, q, c):
                nh = CH[c][1]
                for s in range(SLOTS):
                    sp.dma_start(kpack[q ^ 1][D * s:D * (s + 1), 8 * c:8 * c + nh, :],
                                 k_parts[0:D * nh, c, K_PART[s], bass.ds(TOK2 * (j + 1), TOK2)]).then_inc(d_kpack[c], 16)
                need(sp, q_low, 3 * (j + 1) + c + 1)
                for s in range(SLOTS):
                    sp.dma_start(qpack[q ^ 1][D * s:D * (s + 1), 8 * c:8 * c + nh, :],
                                 q_parts[0:D * nh, c, Q_PART[s], :]).then_inc(d_qpack[c], 16)

            def sem_row(q):
                sp.dma_start(qpack[q ^ 1][R_SEM:R_SEM + 1, :, :],
                             sem_low[2 * N - 1:2 * N, :].unsqueeze(1).broadcast_to((1, H, Q2))).then_inc(d_semrow, 16)

            for c in range(3):
                pack(-1, 1, c)
            sp.wait_ge(k_mm, 6)
            sp.dma_start(ctx_g[1], ctxT[6:8].rearrange("g p k t -> p g k t")).then_inc(d_ctx_g[1], 16)
            sp.wait_ge(q_mm, 3)
            sp.dma_start(xT_sb[:], xT[1].rearrange("c p q -> p c q")).then_inc(d_xT, 16)
            sp.dma_start(ctx_sb[1][:], ctxT[1]).then_inc(d_ctx, 16)
            sp.wait_ge(s_low, 1)
            sem_row(1)
            sp.wait_ge(k_low, 3 * GROUPS)

            def iteration(j, q, fin, old, cur, nxt):
                more = nxt and (not isinstance(j, int) or j + 2 < PAIRS)
                if fin:
                    need(sp, o_done, TILES * (j - 1))
                    sp.dma_start(out[j - 2], ob).then_inc(d_out, 16)
                if old:
                    sp.dma_start(xr_sb[:], xr[j - 1]).then_inc(d_xr, 16)
                if cur:
                    need(sp, v_done, 3 * j + 1)
                    for u in range(2):
                        sp.dma_start(v_sb[q][u][T:TOK], v_ip[N * u:N * (u + 1)]).then_inc(d_v, 16)
                if nxt:
                    for c in range(3):
                        if c == 2:
                            if more:
                                need(sp, q_mm, 3 * (j + 2))
                                sp.dma_start(xT_sb[:], xT[j + 2].rearrange("c p q -> p c q")).then_inc(d_xT, 16)
                            if cur:
                                need(sp, mT_done, j + 1)
                                sp.dma_start(qpack[q][R_MAX:R_ALL, :, :], mT_sb[:, :]).then_inc(d_mrow, 16)
                        if old:
                            sp.wait_ge(st_mm, N_ST * (j - 1) + ST_OF[c])
                        elif cur:
                            sp.wait_ge(last_mm if c == 2 else sq_mm, 1 if c == 2 else 2)
                        pack(j, q, c)
                elif cur:
                    need(sp, mT_done, j + 1)
                    sp.dma_start(qpack[q][R_MAX:R_ALL, :, :], mT_sb[:, :]).then_inc(d_mrow, 16)
                if cur and more:
                    need(sp, v_mm, 3 * (j + 1))
                    sp.dma_start(ctx_sb[q][:], ctxT[j + 2]).then_inc(d_ctx, 16)
                if nxt:
                    need(sp, s_low, j + 2)
                    sem_row(q)

            run(sp, iteration)
            sp.wait_ge(d_out, 16 * PAIRS)

        @block.tensor
        def _(pe):
            def keys(n):
                g, c = divmod(n, 3)
                nr = ROWS[c]
                pe.wait_ge(d_ctx_g[g % 2], 16 * (g // 2 + 1))
                if n >= 2:
                    pe.wait_ge(k_rs, n - 1)
                ps = ST[n % 2][0:nr, 0:GB * TOK].rearrange("p (g b t) -> p g b t", g=2, b=2)
                for w, there, t0, t1, c0, c1 in ((wk_sb, d_wk, 0, T, 0, IP0), (wkip_sb, d_wkip, T, TOK, IP0, TOK2)):
                    if n == 0:
                        pe.wait_ge(there, 16 * KC)
                    cg = ctx_g[g % 2][:, :, :, c0:c1].rearrange("p g k (b t) -> p g k b t", b=2)
                    for k in range(KC):
                        mm = pe.matmul(ps[:, :, :, t0:t1], w[:, k, P * c:P * c + nr], cg[:, :, k, :, :],
                                       start=(k == 0), stop=(k == KC - 1), skip_group_check=True)
                mm.then_inc(k_mm, 1)

            def queries(j, c):
                nr = ROWS[c]
                if c == 0:
                    pe.wait_ge(d_xT, 16 * (j + 2))
                    need(pe, v_done, 3 * j)
                else:
                    need(pe, q_rs, 3 * (j + 1) + c)
                for k in range(3):
                    mm = pe.matmul(PJ[1][0:nr, :], wq_sb[:, k, P * c:P * c + nr], xT_sb[:, k, :],
                                   start=(k == 0), stop=(k == 2))
                mm.then_inc(q_mm, 1)

            def values(j, q, i, nxt):
                if i == 0:
                    need(pe, s_rest, j + 1)
                elif i == 1:
                    need(pe, q_rs, 3 * min(j + 2, PAIRS) if isinstance(j, int) else 3 * (j + 2))
                    need(pe, g_done, 2 * min(j + 2, PAIRS) if isinstance(j, int) else 2 * (j + 2))
                    need(pe, v_done, 3 * j)
                elif nxt:
                    need(pe, pT_done, j + 2)
                else:
                    need(pe, v_done, 3 * j + 2)
                b = PJ[1 if i else 0]
                t0, t1 = (T * (i - 1), T * i) if i else (IP0, TOK2)
                for k in range(KC):
                    mm = pe.matmul(b[0:t1 - t0, 0:C], ctx_sb[q][:, k, t0:t1], wv_sb[:, k, 0 if i else 1, :],
                                   start=(k == 0), stop=(k == KC - 1))
                mm.then_inc(v_mm, 1)

            def token_products(j, q):
                pe.wait_ge(d_ctx, 16 * (j + 2))
                need(pe, q_rs, 3 * (j + 2))
                for u in range(2):
                    for k in range(KC):
                        mm = pe.matmul(PJ[1][0:T, N * u:N * (u + 1)], ctx_sb[q ^ 1][:, k, T * u:T * (u + 1)],
                                       ctx_sb[q ^ 1][:, k, IP0 + N * u:IP0 + N * (u + 1)], start=(k == 0),
                                       stop=(k == KC - 1), skip_group_check=True)
                mm.then_inc(g_mm, 1)

            def text_logits(j, chunks, fin, cur):
                if chunks[0] == 0 and cur:
                    need(pe, v_done, 3 * j + 1)
                if chunks[0] == 0 and fin:
                    need(pe, o_done, TILES * (j - 1))
                if chunks[0] == 0:
                    need(pe, s_rest, j + 1)
                for c in chunks:
                    need(pe, q_low, 3 * (j + 1) + c + 1)
                    for t in range(TILES):
                        for a, b in zip(Q_PART, K_PART):
                            mm = pe.matmul(PJ[0][:, T * t:T * (t + 1)], q_parts[:, c, a, P * t:P * (t + 1)],
                                           k_parts[:, c, b, bass.ds(TOK2 * (j + 1) + TOK * (t // 2), T)],
                                           start=(t == 0 and c == 0 and a + b == 0),
                                           stop=(c == 2 and a == 2), skip_group_check=True)
                if chunks[-1] == 2:
                    mm.then_inc(l_mm, 1)

            def text_probs_T(j, cur):
                if cur:
                    need(pe, v_done, 3 * j + 2)
                need(pe, l_normed, j + 2)
                need(pe, g_done, 2 * (j + 2))
                for t in range(TILES):
                    mm = pe.transpose(PJ[1][0:T, P * t:P * (t + 1)], l_exp[:, t, :], ident)
                mm.then_inc(pT_mm, 1)

            def semantic(j):
                need(pe, pT_done, j + 2)
                need(pe, l_exped, TILES * (j + 2))
                for u in range(2):
                    mm = pe.matmul(PJ[0][:, S * u:S * (u + 1)], g_sb[u][:].rearrange("p r n -> p (r n)")[:, 0:P],
                                   pT_sb[:, S * u:S * (u + 1)], start=True, stop=True, skip_group_check=True)
                mm.then_inc(sem_mm, 1)

            def logits(j, q, t, g, b):
                for i in range(HG):
                    pe.matmul(b[:, LH * i:LH * i + TOK], qpack[q][0:R_QK, HG * g + i, P * t:P * (t + 1)],
                              kpack[q][0:R_QK, HG * g + i, TOK * (t // 2):TOK * (t // 2 + 1)],
                              start=(i == 0), stop=False, skip_group_check=True)
                ip = b[:, :].rearrange("p (h t) -> p h t", t=LH)[:, :, T:TOK]
                return pe.matmul(ip, sempack[q][:, P * t:P * (t + 1)], sel_q.rearrange("p (h n) -> p h n", h=HG),
                                 start=False, stop=True, skip_group_check=True)

            def rows(j, q, r):
                t, k = divmod(r, 2)
                if r == 0:
                    need(pe, s_pack, j + 1)
                    need(pe, mT_done, j)
                if t == 0:
                    pe.wait_ge(d_kpack[k], D_PACK * (j + 1))
                    pe.wait_ge(d_qpack[k], D_PACK * (j + 1))
                need(pe, sq_sub, LAST_SUM * j + r)
                logits(j, q, t, 2 * k, SQ[0])
                logits(j, q, t, 2 * k + 1, SQ[1]).then_inc(sq_mm, 1)

            def last_rows(j, q, t, fin):
                if t == 0:
                    pe.wait_ge(d_kpack[2], D_PACK * (j + 1))
                    pe.wait_ge(d_qpack[2], D_PACK * (j + 1))
                if fin and t == 0:
                    need(pe, o_done, TILES * (j - 2) + 2)
                need(pe, sq_acc, TILES * j + t)
                logits(j, q, t, G - 1, LG).then_inc(last_mm, 1)

            def maxima_T(j):
                need(pe, m_split, j + 1)
                need(pe, sq_sub, LAST_SUM * (j + 1))
                for t in range(TILES):
                    mm = pe.transpose(SQ[0].bitcast(BF16)[0:6 * H, P * t:P * (t + 1)],
                                      m_parts[:, t].rearrange("p a k h -> p (a k h)"), ident_b)
                mm.then_inc(mT_mm, 1)

            def columns(j, q, n):
                g, u = STEPS[n]
                if n == 0:
                    need(pe, d_mrow, 16 * j)
                    need(pe, d_semrow, 16 * j)
                for i in range(2):
                    need(pe, exped, N_ST * (j - 1) + 2 * n + i - 1)
                    pe.matmul(ST[i][0:TOK, :].rearrange("p (h q) -> p h q", h=2), sel_t,
                              sempack[q ^ 1][:, S * u:S * (u + 1)].unsqueeze(1).broadcast_to((P, 2, S)),
                              start=True, stop=False, skip_group_check=True)
                    for k in range(2):
                        h = HG * g + 2 * i + k
                        mm = pe.matmul(ST[i][0:TOK, S * k:S * (k + 1)], kpack[q ^ 1][:, h, TOK * u:TOK * (u + 1)],
                                       qpack[q ^ 1][:, h, S * u:S * (u + 1)],
                                       start=False, stop=(k == 1), skip_group_check=True)
                    mm.then_inc(st_mm, 1)

            def value_products(j, q, n):
                g, u = STEPS[n]
                c, e = divmod(g, 2)
                need(pe, masked, N_PV * (j - 1) + n + 1)
                if n == 0:
                    need(pe, d_v, 16 * 2 * j)
                    need(pe, v_done, 3 * j)
                if e == 0:
                    need(pe, hs_done, 2 * CHUNKS * (j - 1) + 2 * c + u)
                for i in range(HG):
                    mm = pe.matmul(NU[32 * i:32 * (i + 1), 0:S], v_sb[q ^ 1][u][:, e, HG * c + i, :], pt[n % 2][:, i, :],
                                   start=(e == 0), stop=(n in NUMS_AT), skip_group_check=True)
                mm.then_inc(pv_mm, 1)

            def project(j, t, cur):
                if t == 0:
                    need(pe, hs_done, 2 * CHUNKS * (j - 1))
                    if not isinstance(j, int) or j <= PAIRS:
                        need(pe, sq_acc, TILES * j)
                b = output_bank(j, t)
                if t == 2 and cur:
                    need(pe, v_done, 3 * j + 1)
                if t == 0 and not cur or t and b is output_bank(j, t - 1):
                    need(pe, o_done, TILES * (j - 2) + t)
                for c in range(CHUNKS):
                    mm = pe.matmul(b[:, 0:C], hs[:, c, P * t:P * (t + 1)], wout_sb[:, c, :],
                                   start=(c == 0), stop=(c == CHUNKS - 1))
                mm.then_inc(o_mm, 1)

            n = 0
            for item in START:
                if item == "K":
                    keys(n)
                    n += 1
                elif item[0] == "Q":
                    if item == "Q0":
                        pe.wait_ge(d_wq, 16)
                    queries(-1, int(item[1]))
                elif item == "G":
                    token_products(-1, 1)
                elif item == "L":
                    pe.wait_ge(k_low, 3)
                    pe.wait_ge(parts_zero, 2)
                    text_logits(-1, (0, 1, 2), False, False)
                elif item == "P":
                    pe.wait_ge(d_const, 16 * 6)
                    text_probs_T(-1, False)
                elif item == "S":
                    semantic(-1)
            pe.wait_ge(d_w, 16 * (1 + KC))

            def iteration(j, q, fin, old, cur, nxt):
                if isinstance(j, int) and j == 1:
                    pe.wait_ge(k_low, 3 * GROUPS)
                for n in range(N_PV):
                    if fin and n == PROJECT_AT[0]:
                        project(j, 0, cur)
                    if cur and n in PAIR_AT:
                        rows(j, q, PAIR_AT.index(n))
                    if nxt and n == QUERIES_AT[0]:
                        queries(j, 0)
                    if old:
                        columns(j, q, n)
                    if fin and n in PROJECT_AT[1:]:
                        project(j, PROJECT_AT.index(n), cur)
                    if nxt and n == SEM_AT:
                        semantic(j)
                    if old and n == N_PV - 1:
                        value_products(j, q, n - 1)
                    if cur and n in VALUES_AT:
                        values(j, q, VALUES_AT.index(n), nxt)
                    if nxt and n in QUERIES_AT[1:]:
                        queries(j, QUERIES_AT.index(n))
                    if nxt and n == G_AT:
                        token_products(j, q)
                    if cur and n in LAST_AT:
                        last_rows(j, q, LAST_AT.index(n), fin)
                    if nxt and n == L_AT - 1:
                        text_logits(j, (0, 1), fin, cur)
                    if nxt and n == L_AT:
                        text_logits(j, (2,), fin, cur)
                    if nxt and n == PT_AT:
                        text_probs_T(j, cur)
                    if old and 0 < n < N_PV - 1:
                        value_products(j, q, n - 1)
                if old:
                    value_products(j, q, N_PV - 1)
                if cur:
                    maxima_T(j)

            run(pe, iteration)

        @block.scalar
        def _(act):
            act.preload_act_table_set("natural_log_exp_and_others")
            def keys(n):
                g, c = divmod(n, 3)
                nr, at = ROWS[c], slice(GB * TOK * g, GB * TOK * (g + 1))
                act.wait_ge(k_mm, n + 1)
                act.activation(k_parts[0:nr, c, 0, at], ST[n % 2][0:nr, 0:GB * TOK], ACT.Copy).then_inc(k_hi, 1)
                act.wait_ge(k_rs, n + 1)
                act.activation(k_parts[0:nr, c, 1, at], k_rest[n % 2][0:nr, 0:GB * TOK], ACT.Copy).then_inc(k_mid, 1)

            def q_high(j, c):
                nr = ROWS[c]
                need(act, q_mm, 3 * (j + 1) + c + 1)
                need(act, d_qpack[c], D_PACK * (j + 1))
                need(act, l_mm, j + 1)
                act.activation(q_parts[0:nr, c, 0, :], PJ[1][0:nr, :], ACT.Copy, scale=SCALE).then_inc(q_hi, 1)

            def q_middle(j, c):
                nr = ROWS[c]
                need(act, q_rs, 3 * (j + 1) + c + 1)
                act.activation(q_parts[0:nr, c, 1, :], rest[c % 2][0:nr, :], ACT.Copy).then_inc(q_mid, 1)

            def softmax_exp(j, n):
                if n >= 2:
                    need(act, pv_mm, N_PV * (j - 1) + n - 1)
                for i in range(2):
                    need(act, st_mm, N_ST * (j - 1) + 2 * n + i + 1)
                    act.activation(pt[n % 2][:, 2 * i:2 * i + 2, :].rearrange("p h q -> p (h q)"), ST[i][0:TOK, :],
                                   ACT.Exp).then_inc(exped, 1)

            def row_exp(j, r):
                need(act, sq_sub, LAST_SUM * j + r + 1)
                act.activation(row_exps[r % 2][:, :, :], row_exps[r % 2][:, :, :], ACT.Exp).then_inc(sq_exp, 1)

            def last_exp(j, t):
                need(act, last_max, TILES * j + t + 1)
                need(act, sq_acc, TILES * j + t)
                for i in range(HG):
                    for kind, t0, t1 in ((0, 0, T), (1, T, TOK)):
                        at = H * t + HG * (G - 1) + i
                        done = act.activation(acc_exps[:, i, t0:t1], LG[:, LH * i + t0:LH * i + t1], ACT.Exp,
                                              bias=m_neg[:, kind, at:at + 1], accum_out=z_sum[:, kind, at:at + 1])
                done.then_inc(sq_acc, 1)

            def products_out(j, n):
                g, u = STEPS[n]
                need(act, pv_mm, N_PV * (j - 1) + n + 1)
                if n == NUMS_AT[0]:
                    need(act, o_mm, TILES * (j - 2) + 2)
                if n == NUMS_AT[1]:
                    need(act, o_mm, TILES * (j - 1))
                act.activation(hs[:, g // 2, S * u:S * (u + 1)], NU[:, 0:S], ACT.Copy).then_inc(hs_done, 1)

            def g_out(j, u):
                need(act, g_mm, j + 2)
                need(act, sem_mm, j + 1)
                act.activation(g_sb[u][:], PJ[1][0:T, N * u:N * (u + 1)].unsqueeze(1).broadcast_to((T, 3, N)), ACT.Copy,
                               scale=SCALE * SEM_SCALE).then_inc(g_done, 1)

            def text_exp(j):
                need(act, l_maxed, j + 2)
                need(act, l_normed, j + 1)
                for t in range(TILES):
                    act.activation(l_exp[:, t, :], PJ[0][:, T * t:T * (t + 1)], ACT.Exp, bias=l_max[:, t:t + 1],
                                   accum_out=l_den[:, t:t + 1]).then_inc(l_exped, 1)

            def text_probs_out(j):
                need(act, pT_mm, j + 2)
                need(act, sem_mm, j + 1)
                act.activation(pT_sb[:, :], PJ[1][0:T, :], ACT.Copy).then_inc(pT_done, 1)

            def sem_high(j):
                need(act, sem_mm, j + 2)
                need(act, s_pack, j + 1)
                need(act, s_low, j + 1)
                act.activation(sem_hi[:, :], PJ[0][:, :], ACT.Copy).then_inc(s_hi, 1)

            def sem_middle(j):
                need(act, s_rest, j + 2)
                act.activation(sem_mid[:, :], sem_rest[:, :], ACT.Copy).then_inc(s_mid, 1)

            n = 0
            for item in START:
                if item == "K":
                    keys(n)
                    n += 1
                elif item[0] == "Q":
                    q_high(-1, int(item[1]))
                    q_middle(-1, int(item[1]))
                elif item == "G":
                    g_out(-1, 0)
                    g_out(-1, 1)
                elif item == "L":
                    text_exp(-1)
                elif item == "P":
                    text_probs_out(-1)
                elif item == "S":
                    sem_high(-1)
                    sem_middle(-1)

            def iteration(j, q, fin, old, cur, nxt):
                for n in range(N_PV):
                    if nxt and n == QUERIES_AT[0]:
                        q_high(j, 0)
                    if old and n - 2 in NUMS_AT:
                        products_out(j, n - 2)
                    if cur and n - 1 in LAST_AT:
                        last_exp(j, LAST_AT.index(n - 1))
                    if old:
                        softmax_exp(j, n)
                    if nxt and n - 1 in QUERIES_AT:
                        q_middle(j, QUERIES_AT.index(n - 1))
                    if nxt and n == L_AT + 1:
                        text_exp(j)
                    if nxt and n == G_AT:
                        g_out(j, 0)
                        g_out(j, 1)
                    if cur and n in PAIR_AT:
                        row_exp(j, PAIR_AT.index(n))
                    if nxt and n in QUERIES_AT[1:]:
                        q_high(j, QUERIES_AT.index(n))
                    if nxt and n == PT_AT:
                        text_probs_out(j)
                    if cur and n == LN_AT:
                        need(act, sq_sum, LAST_SUM * (j + 1))
                        need(act, sq_acc, TILES * (j + 1))
                        need(act, m_split, j)
                        act.activation(z_ln[:, :, :], z_sum[:, :, :], ACT.Ln).then_inc(ln_done, 1)
                    if nxt and n == SEM_AT:
                        sem_high(j)
                    if old and n == N_PV - 1:
                        products_out(j, n - 1)
                    if nxt and n == SEM_AT:
                        sem_middle(j)
                if old:
                    products_out(j, N_PV - 1)
                if cur:
                    need(act, mT_mm, j + 1)
                    need(act, d_mrow, 16 * j)
                    act.activation(mT_sb[:, :], SQ[0].bitcast(BF16)[0:6 * H, 0:Q2], ACT.Copy).then_inc(mT_done, 1)

            run(act, iteration)

        @block.vector
        def _(dve):
            def keys(n):
                g, c = divmod(n, 3)
                nr = ROWS[c]
                dve.wait_ge(k_hi, n + 1)
                need(dve, k_low, n - 1)
                dve.tensor_tensor(k_rest[n % 2][0:nr, 0:GB * TOK], ST[n % 2][0:nr, 0:GB * TOK],
                                  k_parts[0:nr, c, 0, GB * TOK * g:GB * TOK * (g + 1)], ALU.subtract).then_inc(k_rs, 1)

            def heads(t, g0, g1):
                return slice(H * t + HG * g0, H * t + HG * g1)

            def maxima(b, at, done):
                b = b[:, :].rearrange("p (h t) -> p h t", t=LH)
                dve.tensor_reduce(m_neg[:, 0, at], b[:, :, 0:T], AX_X, ALU.max, negate=True)
                dve.tensor_reduce(m_neg[:, 1, at], b[:, :, T:TOK], AX_X, ALU.max, negate=True).then_inc(done, 1)

            def row_max(j, r):
                t, k = divmod(r, 2)
                need(dve, sq_mm, LAST_SUM * j + r + 1)
                if r == 0:
                    need(dve, m_split, j)
                at = heads(t, 2 * k, 2 * k + 2)
                maxima(SQ2, at, sq_max)
                need(dve, sq_max, LAST_SUM * j + r + 1)
                if r >= 2:
                    need(dve, sq_sum, LAST_SUM * j + r - 1)
                b = SQ2[:, :].rearrange("p (h t) -> p h t", t=LH)
                for kind, t0, t1 in ((0, 0, T), (1, T, TOK)):
                    done = dve.tensor_tensor(row_exps[r % 2][:, :, t0:t1], b[:, :, t0:t1],
                                             m_neg[:, kind, at].unsqueeze(2).broadcast_to((P, 2 * HG, t1 - t0)), ALU.add)
                done.then_inc(sq_sub, 1)

            def last_row_max(j, t):
                need(dve, last_mm, TILES * j + t + 1)
                maxima(LG, heads(t, G - 1, G), last_max)

            def row_sum(j, r):
                t, k = divmod(r, 2)
                need(dve, sq_exp, LAST_SUM * j + r + 1)
                if r == 0:
                    need(dve, ln_done, j)
                at = heads(t, 2 * k, 2 * k + 2)
                dve.tensor_reduce(z_sum[:, 0, at], row_exps[r % 2][:, :, 0:T], AX_X, ALU.add)
                dve.tensor_reduce(z_sum[:, 1, at], row_exps[r % 2][:, :, T:TOK], AX_X, ALU.add).then_inc(sq_sum, 1)

            def split_maxima(j):
                def by_tile(a):
                    return a[:, :, :].rearrange("p k (t h) -> p t k h", t=TILES)
                need(dve, ln_done, j + 1)
                need(dve, mT_mm, j)
                dve.tensor_tensor(m_neg[:, :, :], m_neg[:, :, :], z_ln[:, :, :], ALU.subtract).then_inc(m_step, 1)
                need(dve, m_step, 4 * j + 1)
                dve.tensor_copy(m_parts[:, :, 0], by_tile(m_neg)).then_inc(m_step, 1)
                need(dve, m_step, 4 * j + 2)
                dve.tensor_tensor(by_tile(m_rest), by_tile(m_neg), m_parts[:, :, 0], ALU.subtract).then_inc(m_step, 1)
                need(dve, m_step, 4 * j + 3)
                dve.tensor_copy(m_parts[:, :, 1], by_tile(m_rest)).then_inc(m_step, 1)
                need(dve, m_step, 4 * j + 4)
                dve.tensor_tensor(m_parts[:, :, 2], by_tile(m_rest), m_parts[:, :, 1], ALU.subtract).then_inc(m_split, 1)

            def q_remainder(j, c):
                nr = ROWS[c]
                need(dve, q_hi, 3 * (j + 1) + c + 1)
                need(dve, q_low, 3 * (j + 1) + c - 1)
                dve.scalar_tensor_tensor(rest[c % 2][0:nr, :], PJ[1][0:nr, :], SCALE, q_parts[0:nr, c, 0, :],
                                         ALU.mult, ALU.subtract).then_inc(q_rs, 1)

            def values_out(j, q, i):
                v = v_sb[q][i - 1][0:T] if i else v_ip
                b = PJ[1 if i else 0]
                if i == 0:
                    need(dve, d_v, 16 * 2 * j)
                    need(dve, pv_mm, N_PV * (j - 1))
                need(dve, v_mm, 3 * j + i + 1)
                for e in range(2):
                    n, at = HG * VG[e], HG * VG[0] * D * e
                    done = dve.tensor_copy(v[:, e, 0:n, D * e:D * (e + 1)],
                                           b[0:v.shape[0], at:at + n * D].rearrange("p (h d) -> p h d", d=D))
                done.then_inc(v_done, 1)

            def output(j, t):
                need(dve, xb_done, TILES * (j - 2) + t + 1)
                need(dve, o_mm, TILES * (j - 2) + t + 1)
                dve.tensor_tensor(ob[:, t, :], output_bank(j, t)[:, 0:C], xr_sb[:, t, :], ALU.add).then_inc(o_done, 1)

            def text_max(j):
                need(dve, l_mm, j + 2)
                dve.tensor_reduce(l_max[:, :], PJ[0][:, 0:TILES * T].rearrange("p (t k) -> p t k", t=TILES), AX_X,
                                  ALU.max, negate=True).then_inc(l_maxed, 1)

            def text_norm(j):
                need(dve, l_exped, TILES * (j + 2))
                dve.reciprocal(l_rec[:, :], l_den[:, :]).then_inc(l_recip, 1)
                need(dve, l_recip, j + 2)
                need(dve, pT_mm, j + 1)
                dve.tensor_tensor(l_exp[:, :, :], l_exp[:, :, :],
                                  l_rec[:, :].unsqueeze(2).broadcast_to((P, TILES, T)), ALU.mult).then_inc(l_normed, 1)

            def sem_parts(j, q, old):
                need(dve, s_hi, j + 2)
                need(dve, s_pack, j + 1)
                need(dve, s_low, j + 1)
                dve.scalar_tensor_tensor(sem_rest[:, :], sem_hi[:, :], coef[:, 0:1], PJ[0][:, :], ALU.mult,
                                         ALU.add).then_inc(s_rest, 1)
                need(dve, s_mid, j + 2)
                need(dve, s_rest, j + 2)
                if old:
                    need(dve, st_mm, N_ST * j)
                dve.scalar_tensor_tensor(sempack[q ^ 1][:, :], sem_mid[:, :], coef[:, 1:2], sem_rest[:, :],
                                         ALU.mult, ALU.add).then_inc(s_pack, 1)

            n = 0
            for item in START:
                if item == "K":
                    keys(n)
                    n += 1
                elif item[0] == "Q":
                    q_remainder(-1, int(item[1]))
                elif item == "G":
                    dve.wait_ge(d_const, 16 * 6)
                    dve.tensor_scalar(mask_sb[:, :], mask_raw[:, :], coef[:, 3:4], coef[:, 2:3], ALU.mult,
                                      ALU.add).then_inc(mask_set, 1)
                elif item == "L":
                    text_max(-1)
                    text_norm(-1)
                elif item == "S":
                    sem_parts(-1, 1, False)

            def iteration(j, q, fin, old, cur, nxt):
                for n in range(N_PV):
                    if mask_on_vector(j):
                        mask_probs(dve, j, n)
                    if nxt and n - 1 in QUERIES_AT:
                        q_remainder(j, QUERIES_AT.index(n - 1))
                    if nxt and n == L_AT + 1:
                        text_max(j)
                    if cur and n in PAIR_AT:
                        row_max(j, PAIR_AT.index(n))
                    if cur and n - 1 in PAIR_AT:
                        row_sum(j, PAIR_AT.index(n - 1))
                    if fin and n in PROJECT_AT:
                        output(j, PROJECT_AT.index(n))
                    if nxt and n == L_AT + 1:
                        text_norm(j)
                    if cur and n == LN_AT + 1:
                        split_maxima(j)
                    if nxt and n == SEM_AT:
                        sem_parts(j, q, old)
                    if cur and n in VALUES_AT:
                        values_out(j, q, VALUES_AT.index(n))
                    if cur and n in LAST_AT:
                        last_row_max(j, LAST_AT.index(n))
                    if fin and n == PT_AT:
                        need(dve, d_out, 16 * (j - 1))

            dve.wait_ge(v_zero, 5)
            dve.wait_ge(mask_set, 1)
            run(dve, iteration)

        @block.gpsimd
        def _(pool):
            pool.memset(k_parts[ROWS[2]:P, 2, :, :], 0.0).then_inc(parts_zero, 1)
            pool.memset(q_parts[ROWS[2]:P, 2, :, :], 0.0).then_inc(parts_zero, 1)
            pool.wait_ge(parts_zero, 2)
            for i in range(2):
                for u in range(2):
                    pool.memset(v_sb[i][u][:], 0.0).then_inc(v_zero, 1)
            def keys(n):
                g, c = divmod(n, 3)
                nr, at = ROWS[c], slice(GB * TOK * g, GB * TOK * (g + 1))
                pool.wait_ge(k_mid, n + 1)
                pool.tensor_tensor(k_parts[0:nr, c, 2, at], k_rest[n % 2][0:nr, 0:GB * TOK], k_parts[0:nr, c, 1, at],
                                   ALU.subtract).then_inc(k_low, 1)

            def q_lower(j, c):
                nr = ROWS[c]
                need(pool, q_mid, 3 * (j + 1) + c + 1)
                pool.tensor_tensor(q_parts[0:nr, c, 2, :], rest[c % 2][0:nr, :], q_parts[0:nr, c, 1, :],
                                   ALU.subtract).then_inc(q_low, 1)

            def sem_lower(j):
                need(pool, s_mid, j + 2)
                need(pool, d_semrow, 16 * (j + 1))
                pool.tensor_tensor(sem_low[:, :], sem_rest[:, :], sem_mid[:, :], ALU.subtract).then_inc(s_low, 1)

            n = 0
            for item in START:
                if item == "K":
                    keys(n)
                    n += 1
                elif item[0] == "Q":
                    q_lower(-1, int(item[1]))
                elif item == "S":
                    sem_lower(-1)
            pool.wait_ge(k_mm, 3 * GROUPS)
            pool.memset(v_ip, 0.0).then_inc(v_zero, 1)
            pool.wait_ge(v_zero, 5)
            pool.wait_ge(d_const, 16 * 6)
            pool.wait_ge(mask_set, 1)

            def iteration(j, q, fin, old, cur, nxt):
                for n in range(N_PV):
                    if nxt and n - 1 in QUERIES_AT:
                        q_lower(j, QUERIES_AT.index(n - 1))
                    if old and not mask_on_vector(j):
                        mask_probs(pool, j, n)
                    if nxt and n == SEM_AT:
                        sem_lower(j)
                    if old:
                        for t in range(TILES):
                            if BIAS_AT[t] == n:
                                need(pool, d_xr, 16 * j)
                                pool.tensor_tensor(xr_sb[:, t, :], xr_sb[:, t, :], bias_sb[:, :],
                                                   ALU.add).then_inc(xb_done, 1)

            run(pool, iteration)


def constants():
    import numpy as np

    f = np.zeros((P, C_END), np.float32)
    f[:, C_ID:C_ID + P] = np.eye(P)
    f[N:, C_COEF] = -1.0
    f[2 * N:, C_COEF + 1] = -1.0
    f[0:T, C_COEF + 2] = 1.0
    f[T:, C_COEF + 3] = 1.0

    b = np.zeros((P, B_END), np.float32)
    b[:, B_ID:B_ID + P] = np.eye(P)
    for r in range(P):
        b[r, B_SELT + T + r % N] = 1.0
        for i in range(HG):
            b[r, B_SELQ + N * i + r % N] = 1.0
    k = np.zeros((R_ALL - R_SEM, H, 2, TOK), np.float32)
    k[0, :, :, TOK - 1] = 1.0
    for part in range(3):
        k[1 + 2 * part, :, :, 0:T] = 1.0
        k[2 + 2 * part, :, :, T:TOK] = 1.0
    return f, (b.view(np.uint32) >> 16).astype(np.uint16), (
        k.reshape(-1, H, TOK2).view(np.uint32) >> 16).astype(np.uint16)


def kernel(**inputs):
    import numpy as np
    import concourse.bacc as bacc
    from concourse.bass_utils import run_bass_kernel_spmd

    a = {k: np.asarray(v) for k, v in inputs.items()}

    def by_chunk(w):
        return np.concatenate([w[:, P * c:P * c + D * nh].reshape(-1, nh, D).transpose(0, 2, 1).reshape(-1, D * nh)
                               for c, nh in CH], 1)

    x = a["x"]
    xT = x.reshape(PAIRS, Q2, C).transpose(0, 2, 1)
    xT = np.pad(xT, ((0, 0), (0, 3 * P - C), (0, 0))).reshape(PAIRS, 3, P, Q2)
    xr = x.reshape(PAIRS, TILES, P, C).transpose(0, 2, 1, 3)
    tokens = a["ctx_2048"].reshape(PAIRS, 2, TOK, CD)
    tokens = np.concatenate([tokens[:, :, 0:T].reshape(PAIRS, IP0, CD), tokens[:, :, T:].reshape(PAIRS, 2 * N, CD)], 1)
    ctxT = tokens.reshape(PAIRS, TOK2, KC, P).transpose(0, 3, 2, 1)
    wv = np.stack([a["L0_xattn_Wv"], a["L0_xattn_Wv_ip"]], 1)
    wv = wv.reshape(CD, 2, G, HG * D)
    wv = np.concatenate([wv[:, :, 0::2], wv[:, :, 1::2]], 2)
    wo = np.pad(a["L0_xattn_Wout"].reshape(G, HG, D, C), ((0, 2 * CHUNKS - G), (0, 0), (0, 0), (0, 0)))
    wo = wo.reshape(CHUNKS, 2, HG, D, C).transpose(0, 2, 1, 3, 4).reshape(CHUNKS, P, C)
    f, b, k = constants()
    arrays = {
        "xT": xT, "xr": xr, "ctxT": ctxT, "fside": a["fside_S_0"],
        "wq": np.pad(by_chunk(a["L0_xattn_Wq"]), ((0, 3 * P - C), (0, 0))),
        "wk": by_chunk(a["L0_xattn_Wk"]).reshape(KC, P, C),
        "wkip": by_chunk(a["L0_xattn_Wk_ip"]).reshape(KC, P, C),
        "wv": wv.reshape(KC, P, 2, C), "wout": wo, "bout": a["L0_xattn_bout"],
        "cf": f, "cb": b, "krows": k,
    }
    arrays = {n: np.ascontiguousarray(v) for n, v in arrays.items()}
    nc = bacc.Bacc("TRN2", target_bir_lowering=False, num_devices=1)
    args = [nc.dram_tensor(n, v.shape, mybir.dt.from_np(v.dtype), kind="ExternalInput").ap()
            for n, v in arrays.items()]
    out = nc.dram_tensor("out", (PAIRS, P, TILES, C), F32, kind="ExternalOutput").ap()
    xattn_kernel(nc, *args, out)
    r = run_bass_kernel_spmd(nc, [arrays], core_ids=[0])
    return r.results[0]["out"].transpose(0, 2, 1, 3).reshape(B, S, C)
```
